# Optimizing a Trainium2 kernel written in Bass

```python
import numpy as np
import jax
import jax.numpy as jnp

def _softmax(x, axis=-1):
    return jax.nn.softmax(x, axis=axis)

def _gelu(x):
    return jax.nn.gelu(x, approximate=True)

def _silu(x):
    return jax.nn.silu(x)

def _sigmoid(x):
    return jax.nn.sigmoid(x)

def _layernorm(x, axis=-1, eps=1e-05):
    m = jnp.mean(x, axis=axis, keepdims=True)
    v = jnp.var(x, axis=axis, keepdims=True)
    return (x - m) / jnp.sqrt(v + eps)

def _scatter_add(tgt, idx, src, axis=0):
    return tgt.at[idx].add(src)

def _segment_sum(src, seg, n):
    return jax.ops.segment_sum(src, seg, n)
kernel_name = 'mk_xattn_ffn_d1_seqx_r8_36bf37'

def setup_inputs(seed: int=0):
    np.random.seed(seed)
    _w = jnp.asarray

    def _rec_inputs():
        import jax
        import jax.numpy as jnp
        _rk = jax.random.key(seed)
        x = -0.0002928 + 1 * jax.random.normal(jax.random.fold_in(_rk, 1), (8, 128, 128), jnp.float32)
        _lenS = 128 - jax.random.randint(jax.random.fold_in(_rk, 7), (8,), 0, max(1, 128 // 4) + 1, jnp.int32)
        _lenS2 = 128 - jax.random.randint(jax.random.fold_in(_rk, 8), (8,), 0, max(1, 128 // 4) + 1, jnp.int32)
        _ctx_1024P = jax.random.normal(jax.random.fold_in(_rk, 11), (8, 16, 128), jnp.float32)
        _ctx_1024c = jax.random.dirichlet(jax.random.fold_in(_rk, 511), 0.3 * jnp.ones((16,), jnp.float32), (8, 128))
        _ctx_1024t = jnp.einsum('bsk,bkd->bsd', _ctx_1024c, _ctx_1024P)
        _ctx_1024t = _ctx_1024t * jax.lax.rsqrt(jnp.mean(jnp.square(_ctx_1024t)) + 1e-12) * 0.953939
        ctx_1024 = -1.39393e-06 + 0.999914 * (_ctx_1024t + 0.3 * jax.random.normal(jax.random.fold_in(_rk, 611), (8, 128, 128), jnp.float32))
        _validS = jnp.arange(128)[None, :] < _lenS[:, None]
        _validS2 = jnp.arange(128)[None, :] < _lenS2[:, None]
        _causal = jnp.tril(jnp.ones((128, 128), dtype=bool))
        mask_Bx1xSxS2_bk1 = jnp.broadcast_to(_validS2[:, None, None, :], (8, 1, 128, 128))
        return (x, ctx_1024, mask_Bx1xSxS2_bk1)
    x, ctx_1024, mask_Bx1xSxS2_bk1 = _rec_inputs()

    def _L0_xattn_setup():
        import jax, jax.numpy as jnp
        import numpy as np
        D = 128
        H = 16
        DH = D // H
        B = 2
        S = 256

        def _split_heads(x):
            b, s, _ = x.shape
            return x.reshape(b, s, H, DH).transpose(0, 2, 1, 3)
        key = jax.random.key(seed)
        ks = jax.random.split(key, 12)
        scale = 1.0 / np.sqrt(D)
        inp = {'query': jax.random.normal(ks[0], (B, S, D), jnp.float32), 'key': jax.random.normal(ks[1], (B, S, D), jnp.float32), 'value': jax.random.normal(ks[2], (B, S, D), jnp.float32), 'mask': jax.random.randint(ks[3], (B, 1, S, S), 0, 2).astype(bool), 'Wq': jax.random.normal(ks[4], (D, D), jnp.float32) * scale, 'bq': jnp.zeros((D,), jnp.float32), 'Wk': jax.random.normal(ks[5], (D, D), jnp.float32) * scale, 'bk': jnp.zeros((D,), jnp.float32), 'Wv': jax.random.normal(ks[6], (D, D), jnp.float32) * scale, 'bv': jnp.zeros((D,), jnp.float32), 'Wo': jax.random.normal(ks[7], (D, D), jnp.float32) * scale, 'bo': jnp.zeros((D,), jnp.float32)}
        return inp
    _L0_xattn_all = _L0_xattn_setup()
    _L0_xattn_in = {k: v for k, v in _L0_xattn_all.items() if k in ('Wq', 'bq', 'Wk', 'bk', 'Wv', 'bv', 'Wo', 'bo')}
    del _L0_xattn_all

    def _L0_ffn_setup():
        import jax, jax.numpy as jnp
        import numpy as np
        B, S, H, F, E, K = (2, 256, 128, 512, 8, 2)

        def _init_w(key, shape, fan_in):
            return jax.random.normal(key, shape, jnp.float32) * fan_in ** (-0.5)

        def _ffn(x, wi, bi, wo, bo):
            return jax.nn.selu(x @ wi + bi) @ wo + bo
        key = jax.random.key(seed)
        ks = jax.random.split(key, 6)
        return {'x': jax.random.normal(ks[0], (B, S, H), jnp.float32), 'gate_wi': _init_w(ks[1], (H, F), H), 'gate_bi': jnp.zeros((F,), jnp.float32), 'gate_wo': _init_w(ks[2], (F, H), F), 'gate_bo': jnp.zeros((H,), jnp.float32), 'exp_wi': _init_w(ks[3], (E, H, F), H), 'exp_bi': jnp.zeros((E, F), jnp.float32), 'exp_wo': _init_w(ks[4], (E, F, H), F), 'exp_bo': jnp.zeros((E, H), jnp.float32)}
    _L0_ffn_all = _L0_ffn_setup()
    _L0_ffn_in = {k: v for k, v in _L0_ffn_all.items() if k in ('gate_wi', 'gate_bi', 'gate_wo', 'gate_bo', 'exp_wi', 'exp_bi', 'exp_wo', 'exp_bo')}
    del _L0_ffn_all
    return {'x': x, 'ctx_1024': ctx_1024, 'mask_Bx1xSxS2_bk1': mask_Bx1xSxS2_bk1, 'L0_xattn_Wq': _L0_xattn_in['Wq'], 'L0_xattn_bq': _L0_xattn_in['bq'], 'L0_xattn_Wk': _L0_xattn_in['Wk'], 'L0_xattn_bk': _L0_xattn_in['bk'], 'L0_xattn_Wv': _L0_xattn_in['Wv'], 'L0_xattn_bv': _L0_xattn_in['bv'], 'L0_xattn_Wo': _L0_xattn_in['Wo'], 'L0_xattn_bo': _L0_xattn_in['bo'], 'L0_ffn_gate_wi': _L0_ffn_in['gate_wi'], 'L0_ffn_gate_bi': _L0_ffn_in['gate_bi'], 'L0_ffn_gate_wo': _L0_ffn_in['gate_wo'], 'L0_ffn_gate_bo': _L0_ffn_in['gate_bo'], 'L0_ffn_exp_wi': _L0_ffn_in['exp_wi'], 'L0_ffn_exp_bi': _L0_ffn_in['exp_bi'], 'L0_ffn_exp_wo': _L0_ffn_in['exp_wo'], 'L0_ffn_exp_bo': _L0_ffn_in['exp_bo']}

def reference(x, ctx_1024, mask_Bx1xSxS2_bk1, L0_xattn_Wq, L0_xattn_bq, L0_xattn_Wk, L0_xattn_bk, L0_xattn_Wv, L0_xattn_bv, L0_xattn_Wo, L0_xattn_bo, L0_ffn_gate_wi, L0_ffn_gate_bi, L0_ffn_gate_wo, L0_ffn_gate_bo, L0_ffn_exp_wi, L0_ffn_exp_bi, L0_ffn_exp_wo, L0_ffn_exp_bo):
    import jax
    import jax.numpy as jnp

    def _L0_xattn_ref(query, key, value, mask, Wq, bq, Wk, bk, Wv, bv, Wo, bo):
        import jax, jax.numpy as jnp
        import numpy as np
        D = 128
        H = 16
        DH = D // H
        B = 2
        S = 256

        def _split_heads(x):
            b, s, _ = x.shape
            return x.reshape(b, s, H, DH).transpose(0, 2, 1, 3)
        q = _split_heads(query @ Wq.T + bq)
        k = _split_heads(key @ Wk.T + bk)
        v = _split_heads(value @ Wv.T + bv)
        scores = jnp.einsum('bhqd,bhkd->bhqk', q, k) * (1.0 / np.sqrt(DH))
        scores = jnp.where(mask, jnp.float32(-1000000000.0), scores)
        attn = jax.nn.softmax(scores, axis=-1)
        ctx = jnp.einsum('bhqk,bhkd->bhqd', attn, v)
        ctx = ctx.transpose(0, 2, 1, 3).reshape(query.shape[0], -1, D)
        return ctx @ Wo.T + bo

    def _L0_ffn_ref(x, gate_wi, gate_bi, gate_wo, gate_bo, exp_wi, exp_bi, exp_wo, exp_bo):
        import jax, jax.numpy as jnp
        import numpy as np
        B, S, H, F, E, K = (2, 256, 128, 512, 8, 2)

        def _init_w(key, shape, fan_in):
            return jax.random.normal(key, shape, jnp.float32) * fan_in ** (-0.5)

        def _ffn(x, wi, bi, wo, bo):
            return jax.nn.selu(x @ wi + bi) @ wo + bo
        Bb, Ss, Hh = x.shape
        xf = x.reshape(-1, Hh)
        gate_logits = _ffn(xf, gate_wi, gate_bi, gate_wo, gate_bo)
        topv, topi = jax.lax.top_k(gate_logits, K)
        topv = topv / jnp.sum(topv, axis=-1, keepdims=True)
        onehot = (topi[..., None] == jnp.arange(E)).astype(x.dtype)
        w = jnp.einsum('nk,nke->ne', topv, onehot)
        h = jax.nn.selu(jnp.einsum('nh,ehf->enf', xf, exp_wi) + exp_bi[:, None, :])
        out_e = jnp.einsum('enf,efh->enh', h, exp_wo) + exp_bo[:, None, :]
        out = jnp.einsum('enh,ne->nh', out_e, w)
        return out.reshape(Bb, Ss, Hh)
    x = x + _L0_xattn_ref(_layernorm(x, axis=-1), ctx_1024, ctx_1024, mask_Bx1xSxS2_bk1, L0_xattn_Wq, L0_xattn_bq, L0_xattn_Wk, L0_xattn_bk, L0_xattn_Wv, L0_xattn_bv, L0_xattn_Wo, L0_xattn_bo)
    x = x + _L0_ffn_ref(_layernorm(x, axis=-1), L0_ffn_gate_wi, L0_ffn_gate_bi, L0_ffn_gate_wo, L0_ffn_gate_bo, L0_ffn_exp_wi, L0_ffn_exp_bi, L0_ffn_exp_wo, L0_ffn_exp_bo)
    return x

_drawn_inputs = setup_inputs


def setup_inputs(seed=0):
    import zlib

    import numpy as np

    out = dict(_drawn_inputs(seed))
    spreads = {'L0_xattn_bq': (0.0, 0.1),
     'L0_xattn_bk': (0.0, 0.8),
     'L0_xattn_bv': (0.0, 0.1),
     'L0_xattn_bo': (0.0, 0.1),
     'L0_ffn_gate_bi': (0.0, 0.1),
     'L0_ffn_gate_bo': (0.0, 0.1),
     'L0_ffn_exp_bi': (0.0, 0.536),
     'L0_ffn_exp_bo': (0.0, 0.536)}
    factors = {}
    for name, (base, spread) in spreads.items():
        noise = np.random.default_rng([zlib.crc32(name.encode()), seed]).standard_normal(out[name].shape)
        drawn = base * np.exp(spread * noise) if base else spread * noise
        out[name] = jnp.asarray(drawn.astype(out[name].dtype))
    for name, factor in factors.items():
        out[name] = (out[name] * factor).astype(out[name].dtype)
    return out
```

```python
import concourse.bass as bass
from concourse import mybir
from contextlib import ExitStack
import math


def pack_columns():
    widths = [("ident", 128), ("before", 128), ("slot_mask", 4), ("iota_j", 64), ("iota_e", 8),
              ("wq3", 384), ("wk3", 384), ("wv", 128), ("wo", 128), ("bq3", 4), ("bk3", 4),
              ("bv", 128), ("bo", 128), ("gbo", 128), ("gbi", 4), ("ebi", 32), ("ebo", 512), ("own_e", 96)]
    at, out = 0, {}
    for name, n in widths:
        out[name] = (at, at + n)
        at += n
    return out, at


def xattn_moe(nc, x, ctxT, mask, pack, gwi, gwo, ewi, ewo, out):
    f32, f32r, bf16, f16 = mybir.dt.float32, mybir.dt.float32r, mybir.dt.bfloat16, mybir.dt.float16
    i32, u32, u8 = mybir.dt.int32, mybir.dt.uint32, mybir.dt.uint8
    ALU, ACT, AX = mybir.AluOpType, mybir.ActivationFunctionType, mybir.AxisListType

    B, T, D = 8, 128, 128
    NG, NS, DH = 4, 4, 8
    F, E, J = 512, 8, 64
    FT = F // 128
    NP = E // 2
    KQ, KM = 96, 104
    BIG = float(2.0 ** 32)
    SCALE = 1.0 / math.sqrt(DH)
    EPS = 1e-5
    ALPHA, LAM = 1.6732632423543772848170429916717, 1.0507009873554804934193349852946
    PV = 27

    cols, _ = pack_columns()

    ctx = ExitStack()
    with ctx:
        def sb(name, shape, dt=f32):
            return ctx.enter_context(nc.sbuf_tensor(name, shape, dt))

        def sem(name):
            return ctx.enter_context(nc.semaphore(name))

        X = sb("X", [128, B, D])
        EARLY = sb("EARLY", [128, 4 * B * T])
        CT = EARLY[:, 0:B * T]
        notab = EARLY[:, B * T:2 * B * T]
        xnT = EARLY[:, 2 * B * T:3 * B * T]
        xn = EARLY[:, 3 * B * T:4 * B * T].rearrange("p (b d) -> p b d", b=B)
        HT = EARLY[:, :].rearrange("p (f n) -> p f n", f=FT)
        SM = EARLY[:, 0:2 * B * T].bitcast(bf16).rearrange("p (t a n) -> p t a n", t=B, a=NP)
        HE = EARLY[:, 2 * B * T:4 * B * T].rearrange("p (i a f j) -> p i a f j", i=NP, a=2, f=FT)
        PBUF = sb("PBUF", [128, 3072])
        PF = PBUF[:, 0:1024].rearrange("p (a n) -> p a n", a=2)
        PH = PBUF[:, 1024:2048].bitcast(f16).rearrange("p (a n) -> p a n", a=4)
        PL = PBUF[:, 2048:3072].bitcast(f16).rearrange("p (a n) -> p a n", a=4)
        GM = PBUF[:, 0:2048].bitcast(bf16).rearrange("p (t e j) -> p t e j", t=B, e=E)
        ZB = PBUF[:, 2048:3072].rearrange("p (a n) -> p a n", a=2)
        MK = sb("MK", [128, B, T], u8)
        PK = sb("PK", list(pack.shape))
        GWI = sb("GWI", [128, F])
        GWO = sb("GWO", [128, FT, 128])
        EWI = sb("EWI", [128, E, F])
        EWO = sb("EWO", [128, E, FT, 128])

        def pk(name, rows=128):
            a, b = cols[name]
            return PK[0:rows, a:b]

        maskb = sb("maskb", [128, B, T], bf16)
        identb = sb("identb", [128, 128], bf16)
        negI = sb("negI", [128, 128], bf16)
        beforeb = sb("beforeb", [128, 128], bf16)
        onesb = sb("onesb", [128, 128], bf16)
        full = sb("full", [128, B])
        notfull = sb("notfull", [128, B], bf16)
        xb = sb("xb", [128, B, D])
        st1 = sb("st1", [128, B, 6])
        mv1 = sb("mv1", [128, B, 2])
        rs1 = sb("rs1", [128, B])
        QF2 = sb("QF2", [128, 2, 512])
        QF = QF2[0:KQ, :, :]
        QR = sb("QR", [KM, NG, B * T], f32r)
        KR = sb("KR", [KM, NG, B * T], f32r)
        QX = sb("QX", [KM, 2, NS, NG, T], f32r)
        KX = sb("KX", [KQ, 2, NS, NG, T], f32r)
        VF = sb("VF", [128, 4, 16, DH])
        VT = sb("VT", [128, 4, 16, DH])
        VB = sb("VB", [128, B, 16, PV], bf16)
        NM = sb("NM", [128, 2, 16])
        MB = sb("MB", [128, 2, NG, 2, NS], bf16)
        UN = sb("UN", [128, 16, 9])
        RC = sb("RC", [128, 16])
        AT = sb("AT", [128, 2, 128])
        ATT = sb("ATT", [128, 2, 128])
        x1 = sb("x1", [128, B, D])
        st2 = sb("st2", [128, 6])
        mv2 = sb("mv2", [128, 2])
        rs2 = sb("rs2", [128, 1])
        xn2 = sb("xn2", [128, B, D])
        xn2T = sb("xn2T", [128, B * T])
        XS = sb("XS", [128, 3, B, D], bf16)
        XR = sb("XR", [128, D])
        gb1 = sb("gb1", [128, FT])
        gb2 = sb("gb2", [128, FT])
        lna = sb("lna", [128, 1])
        mhalf = sb("mhalf", [128, B])
        GE = sb("GE", [128, 2, 512])
        GR = sb("GR", [128, 2, 512])
        LG = X
        top8 = sb("top8", [128, B, 8])
        idx8 = sb("idx8", [128, B, 8], u32)
        idxf = sb("idxf", [128, B, 2])
        tsum = sb("tsum", [128, B])
        rsum = sb("rsum", [128, B])
        tw = sb("tw", [128, B, 2])
        oh0 = sb("oh0", [128, B, E])
        oh1 = sb("oh1", [128, B, E])
        selb = sb("selb", [128, B, E], bf16)
        ww = sb("ww", [128, B, E])
        wr = sb("wr", [128, B, E])
        wst = sb("wst", [128, B, 3, E], bf16)
        pos = sb("pos", [128, B, E])
        cmax = sb("cmax", [128, 1])
        nround = sb("nround", [128, 1], i32)
        XG = sb("XG", [128, E * J])
        EE = GE
        RR = GR
        W24 = sb("W24", [24, E * J])
        WM = sb("WM", [128, NP, 24])
        wsl = sb("wsl", [128, NP])
        YF = QF2[:, 0, :].rearrange("p (a d) -> p a d", a=NP)
        YR = QF2[:, 1, :].rearrange("p (a d) -> p a d", a=NP)
        YS = sb("YS", [128, 3, NP, 128], bf16)
        fin = sb("fin", [1, 1])

        bank = [ctx.enter_context(nc.psum_tensor(f"bank{i}", [128, 512], f32)) for i in range(8)]

        (l_pack, l_x, l_mask, l_ctx, l_gate, l_ewi, l_ewo, s_out) = [
            sem(n) for n in ("l_pack", "l_x", "l_mask", "l_ctx", "l_gate", "l_ewi", "l_ewo", "s_out")]
        p_const, p_xb, p_qlo, p_vb, p_pl, p_xs, p_h = [
            sem(n) for n in ("p_const", "p_xb", "p_qlo", "p_vb", "p_pl", "p_xs", "p_h")]
        p_ch, v_ch, v_rr, v_ones = sem("p_ch"), sem("v_ch"), sem("v_rr"), sem("v_ones")
        v_mv1, v_mv2, p_rs1, p_rs2 = sem("v_mv1"), sem("v_mv2"), sem("p_rs1"), sem("p_rs2")
        (v_mask, v_not, v_xn, v_vf, v_klo, v_qf, v_kx, v_qx, v_max, v_mb, v_un, v_at, v_x1, v_xn2,
         v_r, v_lg, v_sel, v_wst, v_n, v_g, v_z, v_h, v_w, v_y, v_acc, v_fin) = [
            sem(n) for n in ("v_mask", "v_not", "v_xn", "v_vf", "v_klo", "v_qf", "v_kx", "v_qx", "v_max", "v_mb",
                             "v_un", "v_at", "v_x1", "v_xn2", "v_r", "v_lg", "v_sel", "v_wst", "v_n", "v_g", "v_z",
                             "v_h", "v_w", "v_y", "v_acc", "v_fin")]
        (a_not, a_xnT, a_kr, a_qr, a_m, a_ph, a_pf, a_at, a_x2, a_e, a_xg, a_w24, a_ee, a_sm) = [
            sem(n) for n in ("a_not", "a_xnT", "a_kr", "a_qr", "a_m", "a_ph", "a_pf", "a_at", "a_x2", "a_e", "a_xg",
                             "a_w24", "a_ee", "a_sm")]
        (t_not, t_xn, t_v, t_k, t_q, t_s, t_m, t_st, t_pv, t_at, t_wo, t_x2, t_z, t_lg, t_pos, t_xg, t_w24, t_tr,
         t_ez, t_wt, t_y, t_sc) = [
            sem(n) for n in ("t_not", "t_xn", "t_v", "t_k", "t_q", "t_s", "t_m", "t_st", "t_pv", "t_at", "t_wo",
                             "t_x2", "t_z", "t_lg", "t_pos", "t_xg", "t_w24", "t_tr", "t_ez", "t_wt", "t_y", "t_sc")]

        def tok(b, n=1):
            return slice(b * T, (b + n) * T)

        def rounds(eng):
            eng.wait_ge(v_n, 1)
            return eng.value_load(nround[0:1, 0:1], min_val=1, max_val=B * T // J)

        LAST = B + 3
        NCONST = 7

        block = ctx.enter_context(nc.Block())

        @block.sync
        def _(sp):
            sp.dma_start(X[:, :, :], x).then_inc(l_x, 16)
            sp.dma_start(MK[:, :, :], mask).then_inc(l_mask, 16)
            sp.dma_start(CT[:, :], ctxT).then_inc(l_ctx, 16)
            sp.dma_start(GWI[:, :], gwi).then_inc(l_gate, 16)
            sp.dma_start(GWO[:, :, :], gwo).then_inc(l_gate, 16)
            sp.dma_start(EWI[:, :, :], ewi).then_inc(l_ewi, 16)
            sp.dma_start(EWO[:, :, :, :], ewo).then_inc(l_ewo, 16)
            sp.wait_ge(v_fin, 1)
            sp.dma_start(out, x1[:, :, :]).then_inc(s_out, 16)
            sp.wait_ge(s_out, 16)

        @block.gpsimd
        def _(pool):
            chain = [0]

            def link(ins):
                chain[0] += 1
                ins.then_inc(p_ch, 1)
                pool.wait_ge(p_ch, chain[0])

            pool.memset(onesb[:, :], 1.0).then_inc(p_const, 1)
            pool.memset(lna[:, :], math.log(ALPHA)).then_inc(p_const, 1)
            link(pool.memset(mhalf[:, :], -0.5))
            link(pool.memset(VB[:, :, :, :], 0.0))
            pool.wait_ge(v_mv1, 1)
            pool.tensor_tensor(rs1[:, :], rs1[:, :], mhalf[:, :], ALU.pow).then_inc(p_rs1, 1)
            pool.memset(VB[:, :, :, DH:DH + 1], 1.0).then_inc(p_const, 1)
            pool.wait_ge(l_pack, 16)
            pool.tensor_copy(identb[:, :], pk("ident")).then_inc(p_const, 1)
            pool.tensor_scalar(negI[:, :], pk("ident"), -BIG, None, ALU.mult).then_inc(p_const, 1)
            pool.tensor_copy(beforeb[:, :], pk("before")).then_inc(p_const, 1)
            pool.tensor_scalar(gb1[:, :], pk("gbi"), math.log(ALPHA), None, ALU.add)
            pool.tensor_scalar(gb2[:, :], pk("gbi"), -ALPHA, None, ALU.add).then_inc(p_const, 1)
            pool.wait_ge(l_x, 16)
            pool.tensor_tensor(xb[:, :, :], X[:, :, :], pk("bo").unsqueeze(1).broadcast_to([128, B, D]),
                               ALU.add).then_inc(p_xb, 1)
            for h in range(2):
                pool.wait_ge(v_vf, h + 1)
                if h == 1:
                    pool.wait_ge(p_qlo, 4)
                vb = VB[:, 4 * h:4 * h + 4, :, :]
                link(pool.tensor_copy(vb[:, :, :, 0:DH], VF[:, :, :, :]))
                link(pool.tensor_tensor(VT[:, :, :, :], VF[:, :, :, :], vb[:, :, :, 0:DH], ALU.subtract))
                link(pool.tensor_copy(vb[:, :, :, 9:9 + DH], VT[:, :, :, :]))
                pool.tensor_tensor(vb[:, :, :, 18:18 + DH], VT[:, :, :, :], vb[:, :, :, 9:9 + DH],
                                   ALU.subtract).then_inc(p_vb, 1)
                for g in range(NG):
                    n = 4 * h + g
                    pool.wait_ge(a_qr, n + 1)
                    pool.wait_ge(p_vb, h + 1)
                    if n >= 1:
                        pool.wait_ge(p_qlo, n)
                    q = QR[0:32, g, tok(4 * h, 4)]
                    pool.tensor_tensor(q, QF[0:32, n % 2, :], q, ALU.subtract).then_inc(p_qlo, 1)
            for b in range(LAST):
                if b < B:
                    for g in range(NG):
                        u = 4 * b + g
                        if u == 0:
                            pool.wait_ge(p_qlo, 8)
                        pool.wait_ge(a_pf, u + 1)
                        if b >= 1:
                            pool.wait_ge(t_pv, u - 3)
                        pool.tensor_tensor(PL[:, g, :], PF[:, u % 2, :], PH[:, g, :], ALU.subtract).then_inc(p_pl, 1)
                if 0 <= b - 2 < B:
                    pool.wait_ge(v_mv2, b - 1)
                    pool.tensor_tensor(rs2[:, :], rs2[:, :], mhalf[:, 0:1], ALU.pow).then_inc(p_rs2, 1)
                c = b - 3
                if c >= 0:
                    pool.wait_ge(v_xn2, c + 1)
                    link(pool.tensor_copy(XS[:, 0, c, :], xn2[:, c, :]))
                    link(pool.tensor_tensor(XR[:, :], xn2[:, c, :], XS[:, 0, c, :], ALU.subtract))
                    link(pool.tensor_copy(XS[:, 1, c, :], XR[:, :]))
                    pool.tensor_tensor(XS[:, 2, c, :], XR[:, :], XS[:, 1, c, :], ALU.subtract).then_inc(p_xs, 1)
                    pool.wait_ge(p_xs, c + 1)
            for n in range(8):
                pool.wait_ge(v_r, n + 1)
                pool.wait_ge(a_e, n + 1)
                link(pool.tensor_scalar(GE[:, n % 2, :], GE[:, n % 2, :], ALPHA, None, ALU.min))
                pool.tensor_tensor(HT[:, n % FT, tok(4 * (n // FT), 4)], GE[:, n % 2, :], GR[:, n % 2, :],
                                   ALU.add).then_inc(p_h, 1)

        @block.scalar
        def _(act):
            act.dma_start(PK[:, :], pack).then_inc(l_pack, 16)
            for h in range(2):
                act.wait_ge(t_not, h + 1)
                act.activation(notab[:, tok(4 * h, 4)], bank[5 + h][:, :], ACT.Copy).then_inc(a_not, 1)
            for h in range(2):
                act.wait_ge(t_xn, h + 1)
                act.activation(xnT[:, tok(4 * h, 4)], bank[4][:, :], ACT.Copy).then_inc(a_xnT, 1)
                for g in range(NG):
                    n = 4 * h + g
                    act.wait_ge(t_k, n + 1)
                    act.activation(KR[0:KQ, g, tok(4 * h, 4)], bank[5][0:KQ, :], ACT.Identity,
                                   bias=pk("bk3", KQ)[:, g:g + 1]).then_inc(a_kr, 1)
                    act.wait_ge(v_qf, n + 1)
                    act.activation(QR[0:KQ, g, tok(4 * h, 4)], QF[:, n % 2, :], ACT.Copy).then_inc(a_qr, 1)

            def max_rows(b):
                act.wait_ge(t_m, b + 1)
                act.activation(QR[KQ:KM, :, tok(b)], bank[5][KQ:KM, :].rearrange("p (g t) -> p g t", g=NG),
                               ACT.Copy).then_inc(a_m, 1)

            max_rows(0)
            for b in range(LAST):
                if b + 1 < B:
                    max_rows(b + 1)
                if 0 <= b - 3 < B:
                    act.wait_ge(t_x2, b - 3 + 1)
                    act.activation(xn2T[:, tok(b - 3)], bank[4][:, 256:384], ACT.Copy).then_inc(a_x2, 1)
                for g in range(NG):
                    if b < B:
                        u = 4 * b + g
                        act.wait_ge(t_st, u + 1)
                        if b >= 1:
                            act.wait_ge(t_pv, u - 3)
                        act.activation(PH[:, g, :], bank[2 + u % 2][:, :], ACT.Exp, scale=SCALE).then_inc(a_ph, 1)
                        if u >= 2:
                            act.wait_ge(p_pl, u - 1)
                        act.activation(PF[:, u % 2, :], bank[2 + u % 2][:, :], ACT.Exp, scale=SCALE).then_inc(a_pf, 1)
                    if g == 0 and 0 <= b - 2 < B:
                        act.wait_ge(t_at, b - 2 + 1)
                        act.activation(ATT[:, b % 2, :], bank[4][:, 0:128], ACT.Copy).then_inc(a_at, 1)
            act.wait_ge(p_const, NCONST)
            for n in range(8):
                act.wait_ge(t_z, n + 1)
                if n >= 2:
                    act.wait_ge(p_h, n - 1)
                act.activation(GE[:, n % 2, :], bank[n % 4][:, :], ACT.Exp,
                               bias=gb1[:, n % FT:n % FT + 1]).then_inc(a_e, 1)
            nr = rounds(act)
            with act.Fori(0, nr) as r:
                act.wait_ge(t_xg, r + 1)
                act.activation(XG[:, :], bank[2][:, :], ACT.Copy).then_inc(a_xg, 1)
                act.wait_ge(t_w24, r + 1)
                act.activation(W24[:, :], bank[0][0:24, :], ACT.Copy).then_inc(a_w24, 1)
                for t in range(B):
                    act.wait_ge(t_tr, r * B + (t + 1))
                    act.activation(SM[:, t, :, :], bank[t % 2][:, 0:256].bitcast(bf16).rearrange(
                        "p (a n) -> p a n", a=NP), ACT.Copy).then_inc(a_sm, 1)
                for i in range(NP):
                    act.wait_ge(v_z, r * NP + (i + 1))
                    if i >= 2:
                        act.wait_ge(v_h, r * NP + (i - 1))
                    act.activation(EE[:, i % 2, :], ZB[:, i % 2, :], ACT.Exp, bias=lna[:, :]).then_inc(a_ee, 1)

        @block.vector
        def _(dve):
            chain = [0]

            def link(ins):
                chain[0] += 1
                ins.then_inc(v_ch, 1)
                dve.wait_ge(v_ch, chain[0])

            dve.memset(KR[KQ:KM, :, :].bitcast(f32), 1.0).then_inc(v_ones, 1)
            dve.wait_ge(l_mask, 16)
            link(dve.tensor_copy(maskb[:, :, :], MK[:, :, :]))
            link(dve.tensor_reduce(full[:, :], maskb[:, :, :], AX.X, ALU.min))
            dve.tensor_scalar(notfull[:, :], full[:, :], -1.0, 1.0, ALU.mult, ALU.add).then_inc(v_not, 1)
            dve.wait_ge(l_x, 16)
            for b in range(B):
                ins = dve.bn_stats(st1[:, b, :], X[:, b, :])
            link(ins)
            for b in range(B):
                ins = dve.bn_aggr(mv1[:, b, :], st1[:, b, :])
            link(ins)
            dve.tensor_scalar(rs1[:, :], mv1[:, :, 1], EPS, None, ALU.add).then_inc(v_mv1, 1)
            dve.wait_ge(p_rs1, 1)
            for b in range(B):
                dve.tensor_scalar(xn[:, b, :], X[:, b, :], mv1[:, b, 0:1], rs1[:, b:b + 1], ALU.subtract,
                                  ALU.mult).then_inc(v_xn, 1)
            dve.wait_ge(l_pack, 16)
            dve.wait_ge(a_not, 2)
            for h in range(2):
                for g in range(NG):
                    n = 4 * h + g
                    dve.wait_ge(t_q, n + 1)
                    if n >= 2:
                        dve.wait_ge(p_qlo, n - 1)
                    dve.scalar_tensor_tensor(out=QF[:, n % 2, :], in0=bank[6][0:KQ, :], scalar=pk("bq3", KQ)[:, g:g + 1],
                                             in1=notab[0:KQ, tok(4 * h, 4)], op0=ALU.add,
                                             op1=ALU.mult).then_inc(v_qf, 1)
                    dve.wait_ge(a_kr, n + 1)
                    k = KR[64:96, g, tok(4 * h, 4)]
                    dve.scalar_tensor_tensor(out=k, in0=bank[5][64:96, :], scalar=pk("bk3")[64:96, g:g + 1], in1=k,
                                             op0=ALU.add, op1=ALU.subtract).then_inc(v_klo, 1)
                    if g == 0:
                        dve.wait_ge(t_v, h + 1)
                        if h == 1:
                            dve.wait_ge(p_vb, 1)
                        dve.tensor_tensor(VF[:, :, :, :].rearrange("p b h d -> p b (h d)"),
                                          bank[4][:, :].rearrange("p (b d) -> p b d", b=4),
                                          pk("bv").unsqueeze(1).broadcast_to([128, 4, 128]),
                                          ALU.add).then_inc(v_vf, 1)

            def expand_keys(b):
                if b == 0:
                    dve.wait_ge(v_klo, 4)
                if b == 4:
                    dve.wait_ge(v_klo, 8)
                if b >= 2:
                    dve.wait_ge(t_s, 4 * (b - 1))
                for s in range(NS):
                    ins = dve.tensor_scalar(KX[:, b % 2, s, :, :], KR[0:KQ, :, tok(b)].bitcast(f32),
                                            pk("slot_mask", KQ)[:, s:s + 1], None, ALU.mult)
                ins.then_inc(v_kx, 1)

            def expand_queries(b):
                dve.wait_ge(a_m, b + 1)
                dve.wait_ge(p_qlo, 4 * (b // 4 + 1))
                if b >= 2:
                    dve.wait_ge(t_st, 4 * (b - 1))
                for s in range(NS):
                    ins = dve.tensor_scalar(QX[:, b % 2, s, :, :], QR[:, :, tok(b)].bitcast(f32),
                                            pk("slot_mask", KM)[:, s:s + 1], None, ALU.mult)
                ins.then_inc(v_qx, 1)

            def row_max(b, g):
                u = 4 * b + g
                dve.wait_ge(t_s, u + 1)
                dve.tensor_reduce(NM[:, b % 2, NS * g:NS * g + NS],
                                  bank[u % 2][:, :].rearrange("p (s k) -> p s k", s=NS), AX.X, ALU.max,
                                  negate=True).then_inc(v_max, 1)

            def split_max(b):
                nm = NM[:, b % 2, :].rearrange("p (g s) -> p g s", g=NG)
                dve.wait_ge(v_max, 4 * b + 4)
                if b >= 2:
                    dve.wait_ge(t_m, b - 1)
                link(dve.tensor_copy(MB[:, b % 2, :, 0, :], nm))
                dve.tensor_tensor(MB[:, b % 2, :, 1, :], nm, MB[:, b % 2, :, 0, :], ALU.subtract).then_inc(v_mb, 1)

            def normalise(b):
                dve.wait_ge(t_pv, 4 * b + 4)
                dve.tensor_reduce(UN[:, :, :], bank[7][:, 0:16 * PV].rearrange("p (h a c) -> p h c a", h=16, a=3),
                                  AX.X, ALU.add).then_inc(v_un, 1)
                dve.wait_ge(v_un, b + 1)
                link(dve.reciprocal(RC[:, :], UN[:, :, DH]))
                dve.tensor_tensor(AT[:, b % 2, :].rearrange("p (h d) -> p h d", h=16), UN[:, :, 0:DH],
                                  RC[:, :].unsqueeze(2).broadcast_to([128, 16, DH]), ALU.mult).then_inc(v_at, 1)

            def second_norm(b):
                dve.wait_ge(t_wo, b + 1)
                if b == 0:
                    dve.wait_ge(p_xb, 1)
                dve.tensor_tensor(x1[:, b, :], bank[4][:, 128:256], xb[:, b, :], ALU.add).then_inc(v_x1, 1)
                dve.wait_ge(v_x1, b + 1)
                link(dve.bn_stats(st2[:, :], x1[:, b, :]))
                link(dve.bn_aggr(mv2[:, :], st2[:, :]))
                dve.tensor_scalar(rs2[:, :], mv2[:, 1:2], EPS, None, ALU.add).then_inc(v_mv2, 1)
                dve.wait_ge(p_rs2, b + 1)
                dve.tensor_scalar(xn2[:, b, :], x1[:, b, :], mv2[:, 0:1], rs2[:, :], ALU.subtract,
                                  ALU.mult).then_inc(v_xn2, 1)

            expand_keys(0)
            expand_keys(1)
            for g in range(NG):
                row_max(0, g)
            split_max(0)
            for g in range(NG):
                row_max(1, g)
            split_max(1)
            expand_keys(2)
            expand_queries(0)
            for b in range(LAST):
                if b + 2 < B:
                    row_max(b + 2, 0)
                if b + 1 < B:
                    expand_queries(b + 1)
                if b + 2 < B:
                    row_max(b + 2, 1)
                if b + 2 < B:
                    row_max(b + 2, 2)
                    row_max(b + 2, 3)
                    split_max(b + 2)
                if b + 3 < B:
                    expand_keys(b + 3)
                if 0 <= b - 2 < B:
                    second_norm(b - 2)
                if 0 <= b - 1 < B:
                    normalise(b - 1)

            for n in range(8):
                dve.wait_ge(a_e, n + 1)
                if n >= 2:
                    dve.wait_ge(p_h, n - 1)
                dve.tensor_scalar(GR[:, n % 2, :], bank[n % 4][:, :], gb2[:, n % FT:n % FT + 1], -ALPHA, ALU.add,
                                  ALU.max).then_inc(v_r, 1)
            for t in range(B):
                dve.wait_ge(t_lg, t + 1)
                dve.scalar_tensor_tensor(out=LG[:, t, :], in0=bank[4 + t % 4][:, 0:128], scalar=LAM, in1=pk("gbo"),
                                         op0=ALU.mult, op1=ALU.add).then_inc(v_lg, 1)
                dve.wait_ge(v_lg, t + 1)
                link(dve.max(top8[:, t, :], LG[:, t, :]))
                ins = dve.max_index(idx8[:, t, :], top8[:, t, :], LG[:, t, :])
            link(ins)
            link(dve.tensor_tensor(tsum[:, :], top8[:, :, 0], top8[:, :, 1], ALU.add))
            link(dve.reciprocal(rsum[:, :], tsum[:, :]))
            link(dve.tensor_tensor(tw[:, :, :], top8[:, :, 0:2], rsum[:, :].unsqueeze(2).broadcast_to([128, B, 2]),
                                   ALU.mult))
            link(dve.tensor_copy(idxf[:, :, :], idx8[:, :, 0:2]))
            iota_e = pk("iota_e").unsqueeze(1).broadcast_to([128, B, E])

            def each(ap):
                return ap.unsqueeze(2).broadcast_to([128, B, E])

            link(dve.tensor_tensor(oh0[:, :, :], iota_e, each(idxf[:, :, 0]), ALU.is_equal))
            link(dve.tensor_tensor(oh1[:, :, :], iota_e, each(idxf[:, :, 1]), ALU.is_equal))
            dve.tensor_tensor(selb[:, :, :], oh0[:, :, :], oh1[:, :, :], ALU.add).then_inc(v_sel, 1)
            link(dve.tensor_tensor(ww[:, :, :], oh0[:, :, :], each(tw[:, :, 0]), ALU.mult))
            link(dve.tensor_tensor(wr[:, :, :], oh1[:, :, :], each(tw[:, :, 1]), ALU.mult))
            link(dve.tensor_tensor(ww[:, :, :], ww[:, :, :], wr[:, :, :], ALU.add))
            link(dve.tensor_copy(wst[:, :, 0, :], ww[:, :, :]))
            link(dve.tensor_tensor(wr[:, :, :], ww[:, :, :], wst[:, :, 0, :], ALU.subtract))
            link(dve.tensor_copy(wst[:, :, 1, :], wr[:, :, :]))
            dve.tensor_tensor(wst[:, :, 2, :], wr[:, :, :], wst[:, :, 1, :], ALU.subtract).then_inc(v_wst, 1)
            dve.wait_ge(t_pos, 2)
            link(dve.scalar_tensor_tensor(out=pos[:, :, :], in0=bank[0][:, 0:B * E].rearrange("p (t e) -> p t e", t=B),
                                          scalar=1.0, in1=selb[:, :, :], op0=ALU.add, op1=ALU.mult))
            link(dve.tensor_scalar(pos[:, :, :], pos[:, :, :], -1.0, None, ALU.add))
            link(dve.tensor_reduce(cmax[:, :], bank[1][:, 0:E], AX.X, ALU.max))
            link(dve.tensor_scalar(cmax[:, :], cmax[:, :], float(J - 1), 1.0 / J, ALU.add, ALU.mult))
            link(dve.tensor_scalar(cmax[:, :], cmax[:, :], 1.0, -(J - 1) / (2.0 * J), ALU.max, ALU.add))
            dve.tensor_copy(nround[:, :], cmax[:, :]).then_inc(v_n, 1)
            nr = rounds(dve)
            with dve.Fori(0, nr) as r:
                for t in range(B):
                    dve.tensor_tensor(GM[:, t, :, :], pos[:, t, :].unsqueeze(2).broadcast_to([128, E, J]),
                                      pk("iota_j").unsqueeze(1).broadcast_to([128, E, J]),
                                      ALU.is_equal).then_inc(v_g, 1)
                dve.wait_ge(v_g, r * B + B)
                dve.tensor_scalar(pos[:, :, :], pos[:, :, :], -float(J), None, ALU.add).then_inc(v_w, 1)

                def biased(i):
                    dve.wait_ge(t_ez, r * NP + (i + 1))
                    dve.tensor_tensor(ZB[:, i % 2, :].rearrange("p (c j) -> p c j", j=J),
                                      bank[4 + i][:, :].rearrange("p (c j) -> p c j", j=J),
                                      pk("ebi")[:, 8 * i:8 * i + 8].unsqueeze(2).broadcast_to([128, 8, J]),
                                      ALU.add).then_inc(v_z, 1)

                def selu(i):
                    dve.wait_ge(v_z, r * NP + (i + 1))
                    if i >= 2:
                        dve.wait_ge(v_h, r * NP + (i - 1))
                    dve.tensor_scalar(RR[:, i % 2, :], ZB[:, i % 2, :], -ALPHA, -ALPHA, ALU.add,
                                      ALU.max).then_inc(v_rr, 1)
                    dve.wait_ge(a_ee, r * NP + (i + 1))
                    dve.wait_ge(v_rr, r * NP + (i + 1))
                    dve.scalar_tensor_tensor(out=HE[:, i, :, :, :].rearrange("p a f j -> p (a f j)"),
                                             in0=EE[:, i % 2, :], scalar=ALPHA, in1=RR[:, i % 2, :], op0=ALU.min,
                                             op1=ALU.add).then_inc(v_h, 1)

                biased(0)
                biased(1)
                selu(0)
                biased(2)
                selu(1)
                biased(3)
                selu(2)
                selu(3)
                dve.wait_ge(t_wt, r + 1)
                dve.tensor_tensor(WM[:, :, :], bank[0][:, 0:96].rearrange("p (a c) -> p a c", a=NP),
                                  pk("own_e").rearrange("p (a c) -> p a c", a=NP), ALU.mult).then_inc(v_w, 1)
                dve.wait_ge(v_w, r * 6 + 2)
                dve.tensor_reduce(wsl[:, :], WM[:, :, :], AX.X, ALU.add).then_inc(v_w, 1)
                dve.wait_ge(t_y, r + 1)
                dve.scalar_tensor_tensor(out=YF[:, :, :].rearrange("p a d -> p (a d)"), in0=bank[3][:, :], scalar=LAM,
                                         in1=pk("ebo"), op0=ALU.mult, op1=ALU.add).then_inc(v_w, 1)
                dve.wait_ge(v_w, r * 6 + 4)
                dve.tensor_tensor(YF[:, :, :], YF[:, :, :], wsl[:, :].unsqueeze(2).broadcast_to([128, NP, 128]),
                                  ALU.mult).then_inc(v_w, 1)
                dve.wait_ge(v_w, r * 6 + 5)
                dve.tensor_copy(YS[:, 0, :, :], YF[:, :, :]).then_inc(v_y, 1)
                dve.wait_ge(v_y, r * 3 + 1)
                dve.tensor_tensor(YR[:, :, :], YF[:, :, :], YS[:, 0, :, :], ALU.subtract).then_inc(v_w, 1)
                dve.wait_ge(v_w, r * 6 + 6)
                dve.tensor_copy(YS[:, 1, :, :], YR[:, :, :]).then_inc(v_y, 1)
                dve.wait_ge(v_y, r * 3 + 2)
                dve.tensor_tensor(YS[:, 2, :, :], YR[:, :, :], YS[:, 1, :, :], ALU.subtract).then_inc(v_y, 1)
                for t in range(B):
                    dve.wait_ge(t_sc, r * B + (t + 1))
                    dve.tensor_tensor(x1[:, t, :], bank[4 + t % 4][:, 0:128], x1[:, t, :], ALU.add).then_inc(v_acc, 1)
                dve.wait_ge(v_acc, r * B + B)
            dve.memset(fin[:, :], 0.0).then_inc(v_fin, 1)

        @block.tensor
        def _(pe):
            pe.wait_ge(p_const, NCONST)
            pe.wait_ge(v_not, 1)
            for h in range(2):
                for b in range(4):
                    mm = pe.matmul(bank[5 + h][:, tok(b)], notfull[:, 4 * h + b:4 * h + b + 1].broadcast_to([128, 128]),
                                   identb[:, :], start=True, stop=True)
                mm.then_inc(t_not, 1)
            pe.wait_ge(l_ctx, 16)
            for h in range(2):
                if h == 1:
                    pe.wait_ge(v_vf, 1)
                pe.wait_ge(v_xn, 4 * h + 4)
                for b in range(4):
                    mm = pe.transpose(bank[4][:, tok(b)], xn[:, 4 * h + b, :], pk("ident"))
                mm.then_inc(t_xn, 1)
                for g in range(NG):
                    n = 4 * h + g
                    if n == 0:
                        pe.wait_ge(a_not, 2)
                    if n >= 1:
                        pe.wait_ge(v_klo, n)
                    pe.matmul(bank[5][0:KQ, :], pk("wk3")[:, g * KQ:g * KQ + KQ], CT[:, tok(4 * h, 4)],
                              start=True, stop=True).then_inc(t_k, 1)
                    if g == 0:
                        pe.wait_ge(a_xnT, h + 1)
                        for b in range(4):
                            mm = pe.matmul(bank[4][:, tok(b)], CT[:, tok(4 * h + b)], pk("wv"), start=True, stop=True)
                        mm.then_inc(t_v, 1)
                    if n >= 1:
                        pe.wait_ge(v_qf, n)
                    pe.matmul(bank[6][0:KQ, :], pk("wq3")[:, g * KQ:g * KQ + KQ], xnT[:, tok(4 * h, 4)],
                              start=True, stop=True).then_inc(t_q, 1)

            def scores(b, g):
                u = 4 * b + g
                if g == 0:
                    pe.wait_ge(v_kx, b + 1)
                    pe.wait_ge(p_qlo, 4 * (b // 4 + 1))
                if u >= 2:
                    pe.wait_ge(v_max, u - 1)
                pe.matmul(bank[u % 2][:, :], negI[:, :], maskb[:, b, :].unsqueeze(1).broadcast_to([128, NS, T]),
                          start=True, stop=False)
                pe.matmul(bank[u % 2][:, :], QR[0:KQ, g, tok(b)], KX[:, b % 2, :, g, :], start=False,
                          stop=True).then_inc(t_s, 1)

            def turned_scores(b, g):
                u = 4 * b + g
                if g == 0:
                    pe.wait_ge(v_qx, b + 1)
                if u >= 2:
                    pe.wait_ge(a_pf, u - 1)
                pe.matmul(bank[2 + u % 2][:, :], maskb[:, b, :], negI[:, :].unsqueeze(1).broadcast_to([128, NS, T]),
                          start=True, stop=False)
                pe.matmul(bank[2 + u % 2][:, :], KR[:, g, tok(b)], QX[:, b % 2, :, g, :], start=False,
                          stop=True).then_inc(t_st, 1)

            def turn_max(b):
                pe.wait_ge(v_mb, b + 1)
                if b >= 1:
                    pe.wait_ge(a_m, b)
                for g in range(NG):
                    mm = pe.matmul(bank[5][KQ:KM, tok(g)], MB[:, b % 2, g, :, :].rearrange("p a s -> p (a s)"),
                                   identb[:, :], start=True, stop=True)
                mm.then_inc(t_m, 1)

            def values(b, g):
                u = 4 * b + g
                pe.wait_ge(p_pl, u + 1)
                if g == 0:
                    pe.wait_ge(p_vb, b // 4 + 1)
                    if b >= 1:
                        pe.wait_ge(v_un, b)
                for s in range(NS):
                    h = NS * g + s
                    o = bank[7][:, h * PV:h * PV + PV]
                    pe.matmul(o, PH[:, g, tok(s)], VB[:, b, h, :], start=True, stop=False)
                    mm = pe.matmul(o, PL[:, g, tok(s)], VB[:, b, h, :], start=False, stop=True)
                mm.then_inc(t_pv, 1)

            for g in range(NG):
                scores(0, g)
            for g in range(NG):
                scores(1, g)
            turn_max(0)
            for b in range(LAST):
                if b + 1 < B:
                    turn_max(b + 1)
                if 0 <= b - 3 < B:
                    pe.wait_ge(v_xn2, b - 3 + 1)
                    pe.transpose(bank[4][:, 256:384], xn2[:, b - 3, :], pk("ident")).then_inc(t_x2, 1)
                for g in range(NG):
                    if b < B:
                        turned_scores(b, g)
                    if b + 2 < B:
                        scores(b + 2, g)
                    if 0 <= b - 1 < B:
                        values(b - 1, g)
                    if g == 0 and 0 <= b - 2 < B:
                        pe.wait_ge(v_at, b - 2 + 1)
                        if b >= 3:
                            pe.wait_ge(a_x2, b - 2)
                        pe.transpose(bank[4][:, 0:128], AT[:, b % 2, :], pk("ident")).then_inc(t_at, 1)
                    if g == 2 and 0 <= b - 2 < B:
                        pe.wait_ge(a_at, b - 2 + 1)
                        pe.matmul(bank[4][:, 128:256], ATT[:, b % 2, :], pk("wo"), start=True,
                                  stop=True).then_inc(t_wo, 1)

            pe.wait_ge(l_gate, 32)
            for n in range(8):
                h, f = n // FT, n % FT
                if f == 0:
                    pe.wait_ge(a_x2, 4 * h + 4)
                if n >= 4:
                    pe.wait_ge(v_r, n - 3)
                pe.matmul(bank[n % 4][:, :], GWI[:, f * 128:f * 128 + 128], xn2T[:, tok(4 * h, 4)], start=True,
                          stop=True).then_inc(t_z, 1)
            for t in range(B):
                pe.wait_ge(p_h, 4 * (t // 4) + 4)
                if t >= 4:
                    pe.wait_ge(v_lg, t - 3)
                for f in range(FT):
                    mm = pe.matmul(bank[4 + t % 4][:, 0:128], HT[:, f, tok(t)], GWO[:, f, :], start=(f == 0),
                                   stop=(f == FT - 1))
                mm.then_inc(t_lg, 1)
            pe.wait_ge(v_sel, 1)
            pe.matmul(bank[0][:, 0:B * E], beforeb[:, :], selb[:, :, :], start=True, stop=True,
                      skip_group_check=True)
            for t in range(B - 1):
                mm = pe.matmul(bank[0][:, (t + 1) * E:B * E], onesb[:, :],
                               selb[:, t, :].unsqueeze(1).broadcast_to([128, B - 1 - t, E]), start=False,
                               stop=True, skip_group_check=True)
            mm.then_inc(t_pos, 1)
            for t in range(B):
                mm = pe.matmul(bank[1][:, 0:E], onesb[:, :], selb[:, t, :], start=(t == 0), stop=(t == B - 1))
            mm.then_inc(t_pos, 1)
            pe.wait_ge(l_ewi, 16)
            pe.wait_ge(l_ewo, 16)
            pe.wait_ge(v_wst, 1)
            pe.wait_ge(p_xs, B)
            nr = rounds(pe)
            with pe.Fori(0, nr) as r:
                for t in range(B):
                    pe.wait_ge(v_g, r * B + (t + 1))
                    g = GM[:, t, :, :].rearrange("p e j -> p (e j)")
                    for part in range(3):
                        mm = pe.matmul(bank[2][:, :], XS[:, part, t, :], g, start=(t == 0 and part == 0),
                                       stop=(t == B - 1 and part == 2))
                mm.then_inc(t_xg, 1)
                for t in range(B):
                    g = GM[:, t, :, :].rearrange("p e j -> p (e j)")
                    mm = pe.matmul(bank[0][0:24, :], wst[:, t, :, :].rearrange("p a e -> p (a e)"), g,
                                   start=(t == 0), stop=(t == B - 1))
                mm.then_inc(t_w24, 1)
                pe.wait_ge(a_w24, r + 1)
                for t in range(B):
                    if t >= 2:
                        pe.wait_ge(a_sm, r * B + (t - 1))
                    for p in range(NP):
                        mm = pe.transpose(bank[t % 2][:, 64 * p:64 * p + 64].bitcast(bf16),
                                          GM[:, t, 2 * p:2 * p + 2, :].rearrange("p e j -> p (e j)"), identb[:, :])
                    mm.then_inc(t_tr, 1)
                pe.wait_ge(a_xg, r + 1)
                for e in range(E):
                    for f in range(FT):
                        c = (e % 2) * 256 + f * J
                        mm = pe.matmul(bank[4 + e // 2][:, c:c + J], EWI[:, e, f * 128:f * 128 + 128],
                                       XG[:, e * J:e * J + J], start=True, stop=True)
                    if e % 2:
                        mm.then_inc(t_ez, 1)
                pe.wait_ge(a_sm, r * B + B)
                for p in range(NP):
                    mm = pe.matmul(bank[0][:, 24 * p:24 * p + 24], W24[:, 128 * p:128 * p + 128],
                                   pk("ident")[0:24, 0:24], start=True, stop=True)
                mm.then_inc(t_wt, 1)
                for e in range(E):
                    if e % 2 == 0:
                        pe.wait_ge(v_h, r * NP + (e // 2 + 1))
                    a = e % 2
                    for f in range(FT):
                        mm = pe.matmul(bank[3][J * a:J * a + J, 128 * (e // 2):128 * (e // 2) + 128],
                                       HE[:, e // 2, a, f, :], EWO[:, e, f, :], start=(f == 0), stop=(f == FT - 1))
                mm.then_inc(t_y, 1)
                pe.wait_ge(v_y, r * 3 + 3)
                for t in range(B):
                    if t >= 4:
                        pe.wait_ge(v_acc, r * B + (t - 3))
                    for p in range(NP):
                        for part in range(3):
                            mm = pe.matmul(bank[4 + t % 4][:, 0:128], SM[:, t, p, :], YS[:, part, p, :],
                                           start=(p == 0 and part == 0), stop=(p == NP - 1 and part == 2))
                    mm.then_inc(t_sc, 1)


def kernel(**inputs):
    import numpy as _np
    import concourse.bacc as _bacc
    from concourse import mybir as _mybir
    from concourse.bass_utils import run_bass_kernel_spmd as _run

    def arr(name):
        return _np.asarray(inputs[name])

    cols, width = pack_columns()
    pack = _np.zeros((128, width), _np.float32)

    def put(name, a):
        lo, hi = cols[name]
        pack[:a.shape[0], lo:hi] = a.reshape(a.shape[0], hi - lo)

    p = _np.arange(128)
    put("ident", _np.eye(128, dtype=_np.float32))
    put("before", _np.triu(_np.ones((128, 128), _np.float32), 1))
    slot = _np.where(p < 96, (p % 32) // 8, p % 4)
    put("slot_mask", (slot[:, None] == _np.arange(4)[None, :]).astype(_np.float32))
    put("iota_j", _np.broadcast_to(_np.arange(64, dtype=_np.float32), (128, 64)))
    put("iota_e", _np.broadcast_to(_np.arange(8, dtype=_np.float32), (128, 8)))
    own = _np.zeros((128, 4, 3, 8), _np.float32)
    for pair in range(4):
        own[p, pair, :, 2 * pair + p // 64] = 1.0
    put("own_e", own)

    def three(wT):
        return _np.broadcast_to(wT.reshape(128, 4, 1, 32), (128, 4, 3, 32))

    def three_b(b):
        return _np.broadcast_to(b.reshape(4, 32).T[None], (3, 32, 4)).reshape(96, 4)

    put("wq3", three(arr("L0_xattn_Wq").T))
    put("wk3", three(arr("L0_xattn_Wk").T))
    put("wv", arr("L0_xattn_Wv").T)
    put("wo", arr("L0_xattn_Wo").T)
    put("bq3", three_b(arr("L0_xattn_bq")))
    put("bk3", three_b(arr("L0_xattn_bk")))
    for name, key in (("bv", "L0_xattn_bv"), ("bo", "L0_xattn_bo"), ("gbo", "L0_ffn_gate_bo")):
        put(name, _np.broadcast_to(arr(key), (128, 128)))
    put("gbi", arr("L0_ffn_gate_bi").reshape(4, 128).T)
    put("ebi", arr("L0_ffn_exp_bi").reshape(8, 4, 128).transpose(2, 0, 1))
    put("ebo", _np.repeat(arr("L0_ffn_exp_bo").reshape(4, 2, 128).transpose(1, 0, 2), 64, axis=0))

    c = _np.ascontiguousarray
    arrays = {
        "in_x": c(arr("x").transpose(1, 0, 2)),
        "in_ctxT": c(arr("ctx_1024").reshape(1024, 128).T),
        "in_mask": c(arr("mask_Bx1xSxS2_bk1").reshape(8, 128, 128).transpose(1, 0, 2)),
        "in_pack": pack,
        "in_gwi": c(arr("L0_ffn_gate_wi")),
        "in_gwo": c(arr("L0_ffn_gate_wo").reshape(4, 128, 128).transpose(1, 0, 2)),
        "in_ewi": c(arr("L0_ffn_exp_wi").transpose(1, 0, 2)),
        "in_ewo": c(arr("L0_ffn_exp_wo").reshape(8, 4, 128, 128).transpose(2, 0, 1, 3)),
    }
    nc = _bacc.Bacc("TRN2", target_bir_lowering=False, num_devices=1)
    args = [nc.dram_tensor(n, a.shape, _mybir.dt.from_np(a.dtype), kind="ExternalInput").ap() for n, a in arrays.items()]
    args.append(nc.dram_tensor("out_0", (128, 8, 128), _mybir.dt.float32, kind="ExternalOutput").ap())
    xattn_moe(nc, *args)
    r = _run(nc, [arrays], core_ids=[0])
    return c(r.results[0]["out_0"].transpose(1, 0, 2))
```

```python
import concourse.bass as bass
from concourse import mybir
from contextlib import ExitStack
import math


def pack_columns():
    widths = [("ident", 128), ("before", 128), ("slot_mask", 4), ("iota_j", 64), ("iota_e", 8),
              ("wq", 128), ("wk", 128), ("wv", 128), ("wo", 128), ("bq", 1), ("bk", 1),
              ("bv", 128), ("bo", 128), ("gbo", 128), ("gbi", 4), ("ebi", 32), ("ebo", 512), ("own_e", 96)]
    at, out = 0, {}
    for name, n in widths:
        out[name] = (at, at + n)
        at += n
    return out, at


def xattn_moe(nc, x, ctxT, mask, pack, gwi, gwo, ewi, ewo, out):
    f32, f32r, bf16, f16 = mybir.dt.float32, mybir.dt.float32r, mybir.dt.bfloat16, mybir.dt.float16
    i32, u32, u8 = mybir.dt.int32, mybir.dt.uint32, mybir.dt.uint8
    ALU, ACT, AX = mybir.AluOpType, mybir.ActivationFunctionType, mybir.AxisListType

    B, T, D = 8, 128, 128
    NG, NS, DH = 4, 4, 8
    F, E, J = 512, 8, 64
    FT = F // 128
    NP = E // 2
    KQ, KM = 96, 104
    BIG = float(2.0 ** 60)
    SCALE = 1.0 / math.sqrt(DH)
    EPS = 1e-5
    ALPHA, LAM = 1.6732632423543772848170429916717, 1.0507009873554804934193349852946
    PV = 27

    cols, _ = pack_columns()

    ctx = ExitStack()
    with ctx:
        def sb(name, shape, dt=f32):
            return ctx.enter_context(nc.sbuf_tensor(name, shape, dt))

        def sem(name):
            return ctx.enter_context(nc.semaphore(name))

        X = sb("X", [128, B, D])
        EARLY = sb("EARLY", [128, 4 * B * T])
        CT = EARLY[:, 0:B * T]
        xnT = EARLY[:, 2 * B * T:3 * B * T]
        xn = EARLY[:, 3 * B * T:4 * B * T].rearrange("p (b d) -> p b d", b=B)
        HT = EARLY[:, :].rearrange("p (f n) -> p f n", f=FT)
        SM = EARLY[:, 0:2 * B * T].bitcast(bf16).rearrange("p (t a n) -> p t a n", t=B, a=NP)
        HE = EARLY[:, 2 * B * T:4 * B * T].rearrange("p (i a f j) -> p i a f j", i=NP, a=2, f=FT)
        PBUF = sb("PBUF", [128, 3072])
        PF = PBUF[:, 0:1024].rearrange("p (a n) -> p a n", a=2)
        PH = PBUF[:, 1024:2048].bitcast(f16).rearrange("p (a n) -> p a n", a=4)
        PL = PBUF[:, 2048:3072].bitcast(f16).rearrange("p (a n) -> p a n", a=4)
        GM = PBUF[:, 0:2048].bitcast(bf16).rearrange("p (t e j) -> p t e j", t=B, e=E)
        ZB = PBUF[:, 2048:3072].rearrange("p (a n) -> p a n", a=2)
        MK = sb("MK", [128, B, T], u8)
        PK = sb("PK", list(pack.shape))
        GWI = sb("GWI", [128, F])
        GWO = sb("GWO", [128, FT, 128])
        EWI = sb("EWI", [128, E, F])
        EWO = sb("EWO", [128, E, FT, 128])

        def pk(name, rows=128):
            a, b = cols[name]
            return PK[0:rows, a:b]

        maskb = sb("maskb", [128, B, T], bf16)
        identb = sb("identb", [128, 128], bf16)
        negI = sb("negI", [128, 128], bf16)
        beforeb = sb("beforeb", [128, 128], bf16)
        onesb = sb("onesb", [128, 128], bf16)
        xb = sb("xb", [128, B, D])
        st1 = sb("st1", [128, B, 6])
        mv1 = sb("mv1", [128, B, 2])
        rs1 = sb("rs1", [128, B])
        HL = sb("HL", [128, 2, 2, 512], f32r)
        PAIR = sb("PAIR", [128, 2, 512])
        QR = sb("QR", [KM, NG, B * T], f32r)
        KR = sb("KR", [KM, NG, B * T], f32r)
        QX = sb("QX", [KM, 2, NS, NG, T], f32r)
        KX = sb("KX", [KQ, 2, NS, NG, T], f32r)
        VF = sb("VF", [128, 4, 16, DH])
        VT = sb("VT", [128, 4, 16, DH])
        VB = sb("VB", [128, B, 16, PV], bf16)
        NM = sb("NM", [128, 2, 16])
        MB = sb("MB", [128, 2, NG, 2, NS], bf16)
        UN = sb("UN", [128, 16, 9])
        RC = sb("RC", [128, 16])
        AT = sb("AT", [128, 2, 128])
        ATT = sb("ATT", [128, 2, 128])
        x1 = sb("x1", [128, B, D])
        st2 = sb("st2", [128, 2, 6])
        mv2 = sb("mv2", [128, 2, 2])
        rs2 = sb("rs2", [128, 2])
        xn2 = sb("xn2", [128, B, D])
        xn2T = sb("xn2T", [128, B * T])
        XS = sb("XS", [128, 3, B, D], bf16)
        XR = sb("XR", [128, 2, D])
        gb1 = sb("gb1", [128, FT])
        gb2 = sb("gb2", [128, FT])
        lna = sb("lna", [128, 1])
        mhalf = sb("mhalf", [128, B])
        GE = sb("GE", [128, 2, 512])
        GR = PAIR
        LG = X
        top8 = sb("top8", [128, B, 8])
        idx8 = sb("idx8", [128, B, 8], u32)
        idxf = sb("idxf", [128, B, 2])
        tsum = sb("tsum", [128, B])
        rsum = sb("rsum", [128, B])
        tw = sb("tw", [128, B, 2])
        oh0 = sb("oh0", [128, B, E])
        oh1 = sb("oh1", [128, B, E])
        selb = sb("selb", [128, B, E], bf16)
        ww = sb("ww", [128, B, E])
        wr = sb("wr", [128, B, E])
        wst = sb("wst", [128, B, 3, E], bf16)
        pos = sb("pos", [128, B, E])
        cmax = sb("cmax", [128, 1])
        nround = sb("nround", [128, 1], i32)
        XG = sb("XG", [128, E * J])
        EE = GE
        RR = GR
        W24 = sb("W24", [24, E * J])
        WM = sb("WM", [128, NP, 24])
        wsl = sb("wsl", [128, NP])
        YF = PAIR[:, 0, :].rearrange("p (a d) -> p a d", a=NP)
        YR = PAIR[:, 1, :].rearrange("p (a d) -> p a d", a=NP)
        YS = sb("YS", [128, 3, NP, 128], bf16)
        fin = sb("fin", [1, 1])

        bank = [ctx.enter_context(nc.psum_tensor(f"bank{i}", [128, 512], f32)) for i in range(8)]

        l_pack, l_x, l_mask, l_ctx, l_gate, l_ewi, l_ewo, s_out = [
            sem(n) for n in ("l_pack", "l_x", "l_mask", "l_ctx", "l_gate", "l_ewi", "l_ewo", "s_out")]
        l_kq = [sem(n) for n in ("l_k0", "l_q0", "l_k1", "l_q1")]
        p_ch, p_rs1, p_ident, p_const, p_xb, p_vb, p_pl, p_xr, p_xs, p_rs2 = [
            sem(n) for n in ("p_ch", "p_rs1", "p_ident", "p_const", "p_xb", "p_vb", "p_pl", "p_xr", "p_xs", "p_rs2")]
        v_ch, v_mv1, v_xn, v_mask, v_lo, v_vf, v_kx, v_qx, v_max, v_mh, v_mb, v_un, v_rc, v_at = [
            sem(n) for n in ("v_ch", "v_mv1", "v_xn", "v_mask", "v_lo", "v_vf", "v_kx", "v_qx", "v_max", "v_mh",
                             "v_mb", "v_un", "v_rc", "v_at")]
        v_x1, v_st2, v_ag2, v_mv2, v_xn2, v_r, v_ht, v_lg, v_top, v_idx, v_sel, v_wst, v_n = [
            sem(n) for n in ("v_x1", "v_st2", "v_ag2", "v_mv2", "v_xn2", "v_r", "v_ht", "v_lg", "v_top", "v_idx",
                             "v_sel", "v_wst", "v_n")]
        v_g, v_z, v_rr, v_h, v_w, v_yf, v_y, v_acc, v_fin = [
            sem(n) for n in ("v_g", "v_z", "v_rr", "v_h", "v_w", "v_yf", "v_y", "v_acc", "v_fin")]
        a_xnT, a_hi, a_kx, a_m, a_ph, a_pf, a_at, a_x2, a_xs, a_e, a_xg, a_w24, a_ee, a_sm = [
            sem(n) for n in ("a_xnT", "a_hi", "a_kx", "a_m", "a_ph", "a_pf", "a_at", "a_x2", "a_xs", "a_e", "a_xg",
                             "a_w24", "a_ee", "a_sm")]
        t_xn, t_v, t_kq, t_s, t_m, t_st, t_pv, t_at, t_wo, t_x2, t_z, t_lg, t_pos = [
            sem(n) for n in ("t_xn", "t_v", "t_kq", "t_s", "t_m", "t_st", "t_pv", "t_at", "t_wo", "t_x2", "t_z",
                             "t_lg", "t_pos")]
        t_xg, t_w24, t_tr, t_ez, t_wt, t_y, t_sc = [
            sem(n) for n in ("t_xg", "t_w24", "t_tr", "t_ez", "t_wt", "t_y", "t_sc")]

        def tok(b, n=1):
            return slice(b * T, (b + n) * T)

        def rounds(eng):
            eng.wait_ge(v_n, 1)
            return eng.value_load(nround[0:1, 0:1], min_val=1, max_val=B * T // J)

        SPREAD = 3 * NG * 16
        LAST = B + 2
        NKA = 3

        block = ctx.enter_context(nc.Block())

        @block.sync
        def _(sp):
            sp.dma_start(X[:, :, :], x).then_inc(l_x, 16)
            sp.dma_start(CT[:, :], ctxT).then_inc(l_ctx, 16)
            sp.dma_start(MK[:, :, :], mask).then_inc(l_mask, 16)

            def spread(n, parts):
                h = n // 2
                sp.wait_ge(v_lo, n + 1)
                dst = QR if n % 2 else KR
                for row, part in enumerate(parts):
                    for g in range(NG):
                        sp.dma_start(dst[32 * row:32 * row + 32, g, tok(4 * h, 4)].bitcast(f32),
                                     HL[32 * g:32 * g + 32, n % 2, part, :].bitcast(f32)).then_inc(l_kq[n], 16)

            for h in range(2):
                spread(2 * h, (0, 0, 1))
                spread(2 * h + 1, (1, 0, 0))
            sp.dma_start(GWI[:, :], gwi).then_inc(l_gate, 16)
            sp.dma_start(GWO[:, :, :], gwo).then_inc(l_gate, 16)
            sp.dma_start(EWI[:, :, :], ewi).then_inc(l_ewi, 16)
            sp.dma_start(EWO[:, :, :, :], ewo).then_inc(l_ewo, 16)
            sp.wait_ge(v_fin, 1)
            sp.dma_start(out, x1[:, :, :]).then_inc(s_out, 16)
            sp.wait_ge(s_out, 16)

        @block.gpsimd
        def _(pool):
            chain = [0]

            def link(ins):
                chain[0] += 1
                ins.then_inc(p_ch, 1)
                pool.wait_ge(p_ch, chain[0])

            pool.memset(mhalf[:, :], -0.5)
            pool.memset(lna[:, :], math.log(ALPHA))
            link(pool.memset(onesb[:, :], 1.0))
            link(pool.memset(KR[KQ:KM, :, :].bitcast(f32), 1.0))
            for h in range(2):
                pool.wait_ge(v_mv1, h + 1)
                rs = rs1[:, 4 * h:4 * h + 4]
                pool.tensor_tensor(rs, rs, mhalf[:, 0:4], ALU.pow).then_inc(p_rs1, 1)
            pool.wait_ge(l_pack, 16)
            pool.tensor_copy(identb[:, :], pk("ident"))
            pool.tensor_scalar(negI[:, :], pk("ident"), -BIG, None, ALU.mult).then_inc(p_ident, 1)
            link(pool.memset(VB[:, :, :, :], 0.0))
            link(pool.memset(VB[:, :, :, DH:DH + 1], 1.0))
            for h in range(2):
                pool.wait_ge(v_vf, h + 1)
                vb = VB[:, 4 * h:4 * h + 4, :, :]
                link(pool.tensor_copy(vb[:, :, :, 0:DH], VF[:, :, :, :]))
                link(pool.tensor_tensor(VT[:, :, :, :], VF[:, :, :, :], vb[:, :, :, 0:DH], ALU.subtract))
                link(pool.tensor_copy(vb[:, :, :, 9:9 + DH], VT[:, :, :, :]))
                pool.tensor_tensor(vb[:, :, :, 18:18 + DH], VT[:, :, :, :], vb[:, :, :, 9:9 + DH],
                                   ALU.subtract).then_inc(p_vb, 1)
                if h == 0:
                    pool.tensor_tensor(xb[:, :, :], X[:, :, :], pk("bo").unsqueeze(1).broadcast_to([128, B, D]),
                                       ALU.add).then_inc(p_xb, 1)
            pool.tensor_scalar(gb1[:, :], pk("gbi"), math.log(ALPHA), None, ALU.add)
            pool.tensor_scalar(gb2[:, :], pk("gbi"), -ALPHA, None, ALU.add)
            pool.tensor_copy(beforeb[:, :], pk("before")).then_inc(p_const, 1)
            for b in range(LAST + 1):
                for g in range(NG):
                    if b < B:
                        u = 4 * b + g
                        pool.wait_ge(a_pf, u + 1)
                        if b >= 1:
                            pool.wait_ge(t_pv, u - 3)
                        pool.tensor_tensor(PL[:, g, :], PF[:, u % 2, :], PH[:, g, :], ALU.subtract).then_inc(p_pl, 1)
                    c = b - 3
                    if c >= 0 and g in (1, 2):
                        pool.wait_ge(a_xs, 2 * c + g)
                        if g == 1:
                            pool.tensor_tensor(XR[:, c % 2, :], xn2[:, c, :], XS[:, 0, c, :],
                                               ALU.subtract).then_inc(p_xr, 1)
                        else:
                            pool.tensor_tensor(XS[:, 2, c, :], XR[:, c % 2, :], XS[:, 1, c, :],
                                               ALU.subtract).then_inc(p_xs, 1)
                if 0 <= b - 2 < B:
                    pool.wait_ge(v_mv2, b - 1)
                    pool.tensor_tensor(rs2[:, b % 2:b % 2 + 1], rs2[:, b % 2:b % 2 + 1], mhalf[:, 0:1],
                                       ALU.pow).then_inc(p_rs2, 1)

        @block.scalar
        def _(act):
            act.dma_start(PK[:, :], pack).then_inc(l_pack, 16)

            def high_part(n, name):
                act.wait_ge(t_kq, n + 1)
                if n >= 2:
                    act.wait_ge(l_kq[n - 2], SPREAD)
                act.activation(HL[:, n % 2, 0, :], bank[5 + n % 2][:, :], ACT.Identity, bias=pk(name)).then_inc(a_hi, 1)

            for h in range(2):
                if h == 0:
                    high_part(0, "bk")
                act.wait_ge(t_xn, h + 1)
                act.activation(xnT[:, tok(4 * h, 4)], bank[4][:, :], ACT.Copy).then_inc(a_xnT, 1)
                if h == 1:
                    high_part(2, "bk")
                high_part(2 * h + 1, "bq")

            def max_rows(b):
                act.wait_ge(t_m, b + 1)
                act.activation(QR[KQ:KM, :, tok(b)], bank[6][KQ:KM, :].rearrange("p (g t) -> p g t", g=NG),
                               ACT.Copy).then_inc(a_m, 1)

            def expand_keys(b, s):
                if s == 0:
                    act.wait_ge(l_kq[2 * (b // 4)], SPREAD)
                    if b >= 2:
                        act.wait_ge(t_s, 4 * (b - 1))
                act.activation(KX[:, b % 2, s, :, :], KR[0:KQ, :, tok(b)].bitcast(f32), ACT.Copy,
                               scale=pk("slot_mask", KQ)[:, s:s + 1]).then_inc(a_kx, 1)

            def gate_exp(n):
                act.wait_ge(t_z, n + 1)
                if n >= 2:
                    act.wait_ge(v_ht, n - 1)
                act.activation(GE[:, n % 2, :], bank[n % 2][:, :], ACT.Exp,
                               bias=gb1[:, n % FT:n % FT + 1]).then_inc(a_e, 1)

            for b in range(2):
                for s in range(NKA):
                    expand_keys(b, s)
            for s in range(NKA):
                expand_keys(2, s)
            max_rows(0)
            for b in range(LAST + 1):
                if b + 1 < B:
                    max_rows(b + 1)
                for g in range(NG):
                    if b < B:
                        u = 4 * b + g
                        act.wait_ge(t_st, u + 1)
                        if b >= 1:
                            act.wait_ge(t_pv, u - 3)
                        act.activation(PH[:, g, :], bank[2 + u % 2][:, :], ACT.Exp, scale=SCALE).then_inc(a_ph, 1)
                        if u >= 2:
                            act.wait_ge(p_pl, u - 1)
                        act.activation(PF[:, u % 2, :], bank[2 + u % 2][:, :], ACT.Exp, scale=SCALE).then_inc(a_pf, 1)
                    if b + 3 < B and g < NKA:
                        expand_keys(b + 3, g)
                    c = b - 3
                    if g == 0 and c >= 0:
                        act.wait_ge(v_xn2, c + 1)
                        act.activation(XS[:, 0, c, :], xn2[:, c, :], ACT.Copy).then_inc(a_xs, 1)
                    if g == 1 and 0 <= b - 2 < B:
                        act.wait_ge(t_at, b - 2 + 1)
                        act.activation(ATT[:, b % 2, :], bank[4][:, 0:128], ACT.Copy).then_inc(a_at, 1)
                    if g == 1 and c >= 0:
                        act.wait_ge(p_xr, c + 1)
                        act.activation(XS[:, 1, c, :], XR[:, c % 2, :], ACT.Copy).then_inc(a_xs, 1)
                    if g == 2 and c >= 0:
                        act.wait_ge(t_x2, c + 1)
                        act.activation(xn2T[:, tok(c)], bank[5][:, tok(c % 4)], ACT.Copy).then_inc(a_x2, 1)
                if b in (7, 8):
                    if b == 7:
                        act.wait_ge(p_const, 1)
                    gate_exp(2 * (b - 7))
                    gate_exp(2 * (b - 7) + 1)
            for n in range(4, 8):
                gate_exp(n)
            nr = rounds(act)
            with act.Fori(0, nr) as r:
                act.wait_ge(t_xg, r + 1)
                act.activation(XG[:, :], bank[2][:, :], ACT.Copy).then_inc(a_xg, 1)
                act.wait_ge(t_w24, r + 1)
                act.activation(W24[:, :], bank[0][0:24, :], ACT.Copy).then_inc(a_w24, 1)
                for i in range(NP):
                    act.wait_ge(v_z, r * NP + (i + 1))
                    if i >= 2:
                        act.wait_ge(v_h, r * NP + (i - 1))
                    act.activation(EE[:, i % 2, :], ZB[:, i % 2, :], ACT.Exp, bias=lna[:, :]).then_inc(a_ee, 1)
                for t in range(B):
                    act.wait_ge(t_tr, r * B + (t + 1))
                    act.activation(SM[:, t, :, :], bank[t % 2][:, 0:256].bitcast(bf16).rearrange(
                        "p (a n) -> p a n", a=NP), ACT.Copy).then_inc(a_sm, 1)

        @block.vector
        def _(dve):
            chain = [0]

            def link(ins):
                chain[0] += 1
                ins.then_inc(v_ch, 1)
                dve.wait_ge(v_ch, chain[0])

            dve.wait_ge(l_x, 16)
            for h in range(2):
                for b in range(4 * h, 4 * h + 4):
                    ins = dve.bn_stats(st1[:, b, :], X[:, b, :])
                link(ins)
                for b in range(4 * h, 4 * h + 4):
                    ins = dve.bn_aggr(mv1[:, b, :], st1[:, b, :])
                link(ins)
                dve.tensor_scalar(rs1[:, 4 * h:4 * h + 4], mv1[:, 4 * h:4 * h + 4, 1], EPS, None,
                                  ALU.add).then_inc(v_mv1, 1)
            for h in range(2):
                dve.wait_ge(p_rs1, h + 1)
                for b in range(4 * h, 4 * h + 4):
                    dve.tensor_scalar(xn[:, b, :], X[:, b, :], mv1[:, b, 0:1], rs1[:, b:b + 1], ALU.subtract,
                                      ALU.mult).then_inc(v_xn, 1)
            dve.wait_ge(l_mask, 16)
            dve.tensor_copy(maskb[:, :, :], MK[:, :, :]).then_inc(v_mask, 1)

            def low_part(n, name):
                dve.wait_ge(a_hi, n + 1)
                dve.scalar_tensor_tensor(out=HL[:, n % 2, 1, :], in0=bank[5 + n % 2][:, :], scalar=pk(name),
                                         in1=HL[:, n % 2, 0, :], op0=ALU.add, op1=ALU.subtract).then_inc(v_lo, 1)

            for h in range(2):
                low_part(2 * h, "bk")
                low_part(2 * h + 1, "bq")
                dve.wait_ge(t_v, h + 1)
                if h == 1:
                    dve.wait_ge(p_vb, 1)
                dve.tensor_tensor(VF[:, :, :, :].rearrange("p b h d -> p b (h d)"),
                                  bank[7][:, :].rearrange("p (b d) -> p b d", b=4),
                                  pk("bv").unsqueeze(1).broadcast_to([128, 4, 128]), ALU.add).then_inc(v_vf, 1)

            def expand_keys(b):
                dve.wait_ge(l_kq[2 * (b // 4)], SPREAD)
                if b >= 2:
                    dve.wait_ge(t_s, 4 * (b - 1))
                for s in range(NKA, NS):
                    dve.tensor_scalar(KX[:, b % 2, s, :, :], KR[0:KQ, :, tok(b)].bitcast(f32),
                                      pk("slot_mask", KQ)[:, s:s + 1], None, ALU.mult).then_inc(v_kx, 1)

            def expand_queries(b, slots):
                if slots[0] == 0:
                    dve.wait_ge(a_m, b + 1)
                    dve.wait_ge(l_kq[1 + 2 * (b // 4)], SPREAD)
                    if b >= 2:
                        dve.wait_ge(t_st, 4 * (b - 1))
                for s in slots:
                    dve.tensor_scalar(QX[:, b % 2, s, :, :], QR[:, :, tok(b)].bitcast(f32),
                                      pk("slot_mask", KM)[:, s:s + 1], None, ALU.mult).then_inc(v_qx, 1)

            def row_max(b, g):
                u = 4 * b + g
                dve.wait_ge(t_s, u + 1)
                dve.tensor_reduce(NM[:, b % 2, NS * g:NS * g + NS],
                                  bank[u % 2][:, :].rearrange("p (s k) -> p s k", s=NS), AX.X, ALU.max,
                                  negate=True).then_inc(v_max, 1)

            def split_max(b, part):
                nm = NM[:, b % 2, :].rearrange("p (g s) -> p g s", g=NG)
                if part == 0:
                    dve.wait_ge(v_max, 4 * b + 4)
                    if b >= 2:
                        dve.wait_ge(t_m, b - 1)
                    dve.tensor_copy(MB[:, b % 2, :, 0, :], nm).then_inc(v_mh, 1)
                else:
                    dve.wait_ge(v_mh, b + 1)
                    dve.tensor_tensor(MB[:, b % 2, :, 1, :], nm, MB[:, b % 2, :, 0, :], ALU.subtract).then_inc(v_mb, 1)

            def normalise(b, step):
                if step == 0:
                    dve.wait_ge(t_pv, 4 * b + 4)
                    if b >= 1:
                        dve.wait_ge(v_at, b)
                    dve.tensor_reduce(UN[:, :, :], bank[7][:, 0:16 * PV].rearrange("p (h a c) -> p h c a", h=16, a=3),
                                      AX.X, ALU.add).then_inc(v_un, 1)
                if step == 1:
                    dve.wait_ge(v_un, b + 1)
                    dve.reciprocal(RC[:, :], UN[:, :, DH]).then_inc(v_rc, 1)
                if step == 2:
                    dve.wait_ge(v_rc, b + 1)
                    dve.tensor_tensor(AT[:, b % 2, :].rearrange("p (h d) -> p h d", h=16), UN[:, :, 0:DH],
                                      RC[:, :].unsqueeze(2).broadcast_to([128, 16, DH]), ALU.mult).then_inc(v_at, 1)

            def second_norm(b, step):
                c = b % 2
                if step == 0:
                    dve.wait_ge(t_wo, b + 1)
                    if b == 0:
                        dve.wait_ge(p_xb, 1)
                    dve.tensor_tensor(x1[:, b, :], bank[4][:, 128:256], xb[:, b, :], ALU.add).then_inc(v_x1, 1)
                if step == 1:
                    dve.wait_ge(v_x1, b + 1)
                    dve.bn_stats(st2[:, c, :], x1[:, b, :]).then_inc(v_st2, 1)
                if step == 2:
                    dve.wait_ge(v_st2, b + 1)
                    dve.bn_aggr(mv2[:, c, :], st2[:, c, :]).then_inc(v_ag2, 1)
                if step == 3:
                    dve.wait_ge(v_ag2, b + 1)
                    dve.tensor_scalar(rs2[:, c:c + 1], mv2[:, c, 1:2], EPS, None, ALU.add).then_inc(v_mv2, 1)
                if step == 4:
                    dve.wait_ge(p_rs2, b + 1)
                    dve.tensor_scalar(xn2[:, b, :], x1[:, b, :], mv2[:, c, 0:1], rs2[:, c:c + 1], ALU.subtract,
                                      ALU.mult).then_inc(v_xn2, 1)

            def gate_selu(n):
                dve.wait_ge(a_e, n + 1)
                if n >= 2:
                    dve.wait_ge(v_ht, n - 1)
                dve.tensor_scalar(GR[:, n % 2, :], bank[n % 2][:, :], gb2[:, n % FT:n % FT + 1], -ALPHA, ALU.add,
                                  ALU.max).then_inc(v_r, 1)
                dve.wait_ge(v_r, n + 1)
                dve.scalar_tensor_tensor(out=HT[:, n % FT, tok(4 * (n // FT), 4)], in0=GE[:, n % 2, :], scalar=ALPHA,
                                         in1=GR[:, n % 2, :], op0=ALU.min, op1=ALU.add).then_inc(v_ht, 1)

            def gate_top(h):
                for t in range(4 * h, 4 * h + 4):
                    dve.wait_ge(t_lg, t + 1)
                    dve.scalar_tensor_tensor(out=LG[:, t, :], in0=bank[6 + t % 2][:, 0:128], scalar=LAM,
                                             in1=pk("gbo"), op0=ALU.mult, op1=ALU.add).then_inc(v_lg, 1)
                for t in range(4 * h, 4 * h + 4):
                    dve.wait_ge(v_lg, t + 1)
                    dve.max(top8[:, t, :], LG[:, t, :]).then_inc(v_top, 1)
                for t in range(4 * h, 4 * h + 4):
                    dve.wait_ge(v_top, t + 1)
                    dve.max_index(idx8[:, t, :], top8[:, t, :], LG[:, t, :]).then_inc(v_idx, 1)

            expand_keys(0)
            expand_keys(1)
            for g in range(NG):
                row_max(0, g)
            split_max(0, 0)
            row_max(1, 0)
            split_max(0, 1)
            for g in range(1, NG):
                row_max(1, g)
            split_max(1, 0)
            expand_keys(2)
            expand_queries(0, (0, 1, 2, 3))
            split_max(1, 1)
            for b in range(LAST):
                if b + 2 < B:
                    row_max(b + 2, 0)
                if b + 1 < B:
                    expand_queries(b + 1, (0, 1))
                if b + 2 < B:
                    row_max(b + 2, 1)
                if b + 1 < B:
                    expand_queries(b + 1, (2, 3))
                if b + 2 < B:
                    row_max(b + 2, 2)
                if b + 3 < B:
                    expand_keys(b + 3)
                if b + 2 < B:
                    row_max(b + 2, 3)
                if 0 <= b - 2 < B:
                    second_norm(b - 2, 0)
                if b + 2 < B:
                    split_max(b + 2, 0)
                if 0 <= b - 2 < B:
                    second_norm(b - 2, 1)
                if b + 2 < B:
                    split_max(b + 2, 1)
                if b in (7, 8):
                    if b == 7:
                        dve.wait_ge(p_const, 1)
                    gate_selu(2 * (b - 7))
                    gate_selu(2 * (b - 7) + 1)
                if 0 <= b - 2 < B:
                    second_norm(b - 2, 2)
                if 0 <= b - 1 < B:
                    normalise(b - 1, 0)
                if 0 <= b - 2 < B:
                    second_norm(b - 2, 3)
                if 0 <= b - 1 < B:
                    normalise(b - 1, 1)
                    normalise(b - 1, 2)
                if 0 <= b - 2 < B:
                    second_norm(b - 2, 4)
                if b == 9:
                    gate_top(0)
            for n in range(4, 8):
                gate_selu(n)
            gate_top(1)
            dve.wait_ge(v_idx, B)
            link(dve.tensor_tensor(tsum[:, :], top8[:, :, 0], top8[:, :, 1], ALU.add))
            link(dve.tensor_copy(idxf[:, :, :], idx8[:, :, 0:2]))
            iota_e = pk("iota_e").unsqueeze(1).broadcast_to([128, B, E])

            def each(ap):
                return ap.unsqueeze(2).broadcast_to([128, B, E])

            dve.tensor_tensor(oh0[:, :, :], iota_e, each(idxf[:, :, 0]), ALU.is_equal)
            link(dve.tensor_tensor(oh1[:, :, :], iota_e, each(idxf[:, :, 1]), ALU.is_equal))
            dve.tensor_tensor(selb[:, :, :], oh0[:, :, :], oh1[:, :, :], ALU.add).then_inc(v_sel, 1)
            link(dve.reciprocal(rsum[:, :], tsum[:, :]))
            link(dve.tensor_tensor(tw[:, :, :], top8[:, :, 0:2], rsum[:, :].unsqueeze(2).broadcast_to([128, B, 2]),
                                   ALU.mult))
            dve.tensor_tensor(ww[:, :, :], oh0[:, :, :], each(tw[:, :, 0]), ALU.mult)
            link(dve.tensor_tensor(wr[:, :, :], oh1[:, :, :], each(tw[:, :, 1]), ALU.mult))
            dve.wait_ge(t_pos, 2)
            link(dve.tensor_reduce(cmax[:, :], bank[1][:, 0:E], AX.X, ALU.max))
            link(dve.scalar_tensor_tensor(out=pos[:, :, :], in0=bank[0][:, 0:B * E].rearrange("p (t e) -> p t e", t=B),
                                          scalar=1.0, in1=selb[:, :, :], op0=ALU.add, op1=ALU.mult))
            link(dve.tensor_scalar(cmax[:, :], cmax[:, :], float(J - 1), 1.0 / J, ALU.add, ALU.mult))
            link(dve.tensor_scalar(cmax[:, :], cmax[:, :], 1.0, -(J - 1) / (2.0 * J), ALU.max, ALU.add))
            dve.tensor_copy(nround[:, :], cmax[:, :]).then_inc(v_n, 1)
            link(dve.tensor_scalar(pos[:, :, :], pos[:, :, :], -1.0, None, ALU.add))
            link(dve.tensor_tensor(ww[:, :, :], ww[:, :, :], wr[:, :, :], ALU.add))
            link(dve.tensor_copy(wst[:, :, 0, :], ww[:, :, :]))
            link(dve.tensor_tensor(wr[:, :, :], ww[:, :, :], wst[:, :, 0, :], ALU.subtract))
            link(dve.tensor_copy(wst[:, :, 1, :], wr[:, :, :]))
            dve.tensor_tensor(wst[:, :, 2, :], wr[:, :, :], wst[:, :, 1, :], ALU.subtract).then_inc(v_wst, 1)
            nr = rounds(dve)
            with dve.Fori(0, nr) as r:
                for t in range(B):
                    dve.tensor_tensor(GM[:, t, :, :], pos[:, t, :].unsqueeze(2).broadcast_to([128, E, J]),
                                      pk("iota_j").unsqueeze(1).broadcast_to([128, E, J]),
                                      ALU.is_equal).then_inc(v_g, 1)
                dve.wait_ge(v_g, r * B + B)
                dve.tensor_scalar(pos[:, :, :], pos[:, :, :], -float(J), None, ALU.add).then_inc(v_w, 1)

                def biased(i):
                    dve.wait_ge(t_ez, r * NP + (i + 1))
                    dve.tensor_tensor(ZB[:, i % 2, :].rearrange("p (c j) -> p c j", j=J),
                                      bank[4 + i][:, :].rearrange("p (c j) -> p c j", j=J),
                                      pk("ebi")[:, 8 * i:8 * i + 8].unsqueeze(2).broadcast_to([128, 8, J]),
                                      ALU.add).then_inc(v_z, 1)

                def selu(i):
                    dve.wait_ge(v_z, r * NP + (i + 1))
                    if i >= 2:
                        dve.wait_ge(v_h, r * NP + (i - 1))
                    dve.tensor_scalar(RR[:, i % 2, :], ZB[:, i % 2, :], -ALPHA, -ALPHA, ALU.add,
                                      ALU.max).then_inc(v_rr, 1)
                    dve.wait_ge(a_ee, r * NP + (i + 1))
                    dve.wait_ge(v_rr, r * NP + (i + 1))
                    dve.scalar_tensor_tensor(out=HE[:, i, :, :, :].rearrange("p a f j -> p (a f j)"),
                                             in0=EE[:, i % 2, :], scalar=ALPHA, in1=RR[:, i % 2, :], op0=ALU.min,
                                             op1=ALU.add).then_inc(v_h, 1)

                biased(0)
                selu(0)
                biased(1)
                selu(1)
                biased(2)
                selu(2)
                biased(3)
                selu(3)
                dve.wait_ge(t_wt, r + 1)
                dve.tensor_tensor(WM[:, :, :], bank[0][:, 0:96].rearrange("p (a c) -> p a c", a=NP),
                                  pk("own_e").rearrange("p (a c) -> p a c", a=NP), ALU.mult).then_inc(v_w, 1)
                dve.wait_ge(v_w, r * 3 + 2)
                dve.tensor_reduce(wsl[:, :], WM[:, :, :], AX.X, ALU.add).then_inc(v_w, 1)
                for k in range(2):
                    dve.wait_ge(t_y, r * 2 + (k + 1))
                    dve.scalar_tensor_tensor(out=YF[:, 2 * k:2 * k + 2, :],
                                             in0=bank[3 - k][:, 0:256].rearrange("p (a d) -> p a d", a=2), scalar=LAM,
                                             in1=pk("ebo").rearrange("p (a d) -> p a d", a=NP)[:, 2 * k:2 * k + 2, :],
                                             op0=ALU.mult, op1=ALU.add).then_inc(v_yf, 1)
                    dve.wait_ge(v_yf, r * 8 + (4 * k + 1))
                    dve.wait_ge(v_w, r * 3 + 3)
                    dve.tensor_tensor(YF[:, 2 * k:2 * k + 2, :], YF[:, 2 * k:2 * k + 2, :],
                                      wsl[:, 2 * k:2 * k + 2].unsqueeze(2).broadcast_to([128, 2, 128]),
                                      ALU.mult).then_inc(v_yf, 1)
                    dve.wait_ge(v_yf, r * 8 + (4 * k + 2))
                    dve.tensor_copy(YS[:, 0, 2 * k:2 * k + 2, :], YF[:, 2 * k:2 * k + 2, :]).then_inc(v_y, 1)
                    dve.wait_ge(v_y, r * 4 + (2 * k + 1))
                    dve.tensor_tensor(YR[:, 2 * k:2 * k + 2, :], YF[:, 2 * k:2 * k + 2, :],
                                      YS[:, 0, 2 * k:2 * k + 2, :], ALU.subtract).then_inc(v_yf, 1)
                    dve.wait_ge(v_yf, r * 8 + (4 * k + 3))
                    dve.tensor_copy(YS[:, 1, 2 * k:2 * k + 2, :], YR[:, 2 * k:2 * k + 2, :]).then_inc(v_yf, 1)
                    dve.wait_ge(v_yf, r * 8 + (4 * k + 4))
                    dve.tensor_tensor(YS[:, 2, 2 * k:2 * k + 2, :], YR[:, 2 * k:2 * k + 2, :],
                                      YS[:, 1, 2 * k:2 * k + 2, :], ALU.subtract).then_inc(v_y, 1)
                for k in range(2):
                    dve.wait_ge(t_sc, r * 2 + (k + 1))
                    dve.tensor_tensor(x1[:, 4 * k:4 * k + 4, :],
                                      bank[4 + k][:, :].rearrange("p (t d) -> p t d", t=4),
                                      x1[:, 4 * k:4 * k + 4, :], ALU.add).then_inc(v_acc, 1)
                dve.wait_ge(v_acc, r * 2 + 2)
            dve.memset(fin[:, :], 0.0).then_inc(v_fin, 1)

        @block.tensor
        def _(pe):
            def project(n):
                h = n // 2
                if n >= 2:
                    pe.wait_ge(v_lo, n - 1)
                if n % 2:
                    pe.wait_ge(a_xnT, h + 1)
                src = xnT if n % 2 else CT
                pe.matmul(bank[5 + n % 2][:, :], pk("wq" if n % 2 else "wk"), src[:, tok(4 * h, 4)],
                          start=True, stop=True).then_inc(t_kq, 1)

            pe.wait_ge(l_pack, 16)
            for h in range(2):
                if h == 0:
                    pe.wait_ge(l_ctx, 16)
                    project(0)
                else:
                    pe.wait_ge(a_xnT, 1)
                pe.wait_ge(v_xn, 4 * h + 4)
                for b in range(4):
                    mm = pe.transpose(bank[4][:, tok(b)], xn[:, 4 * h + b, :], pk("ident"))
                mm.then_inc(t_xn, 1)
                if h == 1:
                    project(2)
                    pe.wait_ge(v_vf, 1)
                for b in range(4):
                    mm = pe.matmul(bank[7][:, tok(b)], CT[:, tok(4 * h + b)], pk("wv"), start=True, stop=True)
                mm.then_inc(t_v, 1)
                project(2 * h + 1)
            pe.wait_ge(p_ident, 1)
            pe.wait_ge(v_mask, 1)

            def scores(b, g):
                u = 4 * b + g
                if u >= 2:
                    pe.wait_ge(v_max, u - 1)
                pe.matmul(bank[u % 2][:, :], negI[:, :], maskb[:, b, :].unsqueeze(1).broadcast_to([128, NS, T]),
                          start=True, stop=False)
                if g == 0:
                    pe.wait_ge(a_kx, NKA * (b + 1))
                    pe.wait_ge(v_kx, (NS - NKA) * (b + 1))
                    pe.wait_ge(l_kq[1 + 2 * (b // 4)], SPREAD)
                pe.matmul(bank[u % 2][:, :], QR[0:KQ, g, tok(b)], KX[:, b % 2, :, g, :], start=False,
                          stop=True).then_inc(t_s, 1)

            def turned_scores(b, g):
                u = 4 * b + g
                if u >= 2:
                    pe.wait_ge(a_pf, u - 1)
                pe.matmul(bank[2 + u % 2][:, :], maskb[:, b, :], negI[:, :].unsqueeze(1).broadcast_to([128, NS, T]),
                          start=True, stop=False)
                if g == 0:
                    pe.wait_ge(v_qx, NS * (b + 1))
                pe.matmul(bank[2 + u % 2][:, :], KR[:, g, tok(b)], QX[:, b % 2, :, g, :], start=False,
                          stop=True).then_inc(t_st, 1)

            def turn_max(b):
                pe.wait_ge(v_mb, b + 1)
                if b >= 1:
                    pe.wait_ge(a_m, b)
                else:
                    pe.wait_ge(v_lo, 4)
                for g in range(NG):
                    mm = pe.matmul(bank[6][KQ:KM, tok(g)], MB[:, b % 2, g, :, :].rearrange("p a s -> p (a s)"),
                                   identb[:, :], start=True, stop=True)
                mm.then_inc(t_m, 1)

            def values(b, g):
                u = 4 * b + g
                pe.wait_ge(p_pl, u + 1)
                if g == 0:
                    pe.wait_ge(p_vb, b // 4 + 1)
                    if b >= 1:
                        pe.wait_ge(v_un, b)
                for s in range(NS):
                    h = NS * g + s
                    o = bank[7][:, h * PV:h * PV + PV]
                    pe.matmul(o, PH[:, g, tok(s)], VB[:, b, h, :], start=True, stop=False)
                    mm = pe.matmul(o, PL[:, g, tok(s)], VB[:, b, h, :], start=False, stop=True)
                mm.then_inc(t_pv, 1)

            def gate_hidden(n):
                h, f = n // FT, n % FT
                if f == 0:
                    pe.wait_ge(a_x2, 4 * h + 4)
                if n >= 2:
                    pe.wait_ge(v_r, n - 1)
                pe.matmul(bank[n % 2][:, :], GWI[:, f * 128:f * 128 + 128], xn2T[:, tok(4 * h, 4)], start=True,
                          stop=True).then_inc(t_z, 1)

            def gate_logits(h):
                for t in range(4 * h, 4 * h + 4):
                    pe.wait_ge(v_ht, 4 * h + 4)
                    if t >= 2:
                        pe.wait_ge(v_lg, t - 1)
                    elif t == 1:
                        pe.wait_ge(v_un, B)
                    for f in range(FT):
                        mm = pe.matmul(bank[6 + t % 2][:, 0:128], HT[:, f, tok(t)], GWO[:, f, :], start=(f == 0),
                                       stop=(f == FT - 1))
                    mm.then_inc(t_lg, 1)

            for g in range(NG):
                scores(0, g)
            for g in range(NG):
                scores(1, g)
            turn_max(0)
            for b in range(LAST + 1):
                if b + 1 < B:
                    turn_max(b + 1)
                for g in range(NG):
                    if b < B:
                        turned_scores(b, g)
                    if b + 2 < B:
                        scores(b + 2, g)
                    if 0 <= b - 1 < B:
                        values(b - 1, g)
                    if g == 1 and 0 <= b - 2 < B:
                        pe.wait_ge(v_at, b - 2 + 1)
                        if b >= 3:
                            pe.wait_ge(v_x1, b - 2)
                        pe.transpose(bank[4][:, 0:128], AT[:, b % 2, :], pk("ident")).then_inc(t_at, 1)
                    if g == 2 and 0 <= b - 2 < B:
                        pe.wait_ge(a_at, b - 2 + 1)
                        pe.matmul(bank[4][:, 128:256], ATT[:, b % 2, :], pk("wo"), start=True,
                                  stop=True).then_inc(t_wo, 1)
                    if g == 2 and 0 <= b - 3 < B:
                        pe.wait_ge(v_xn2, b - 3 + 1)
                        if b - 3 >= 1:
                            pe.wait_ge(a_x2, b - 3)
                        pe.transpose(bank[5][:, tok((b - 3) % 4)], xn2[:, b - 3, :], pk("ident")).then_inc(t_x2, 1)
                if b in (7, 8):
                    if b == 7:
                        pe.wait_ge(l_gate, 32)
                        pe.wait_ge(v_max, 4 * B)
                    gate_hidden(2 * (b - 7))
                    gate_hidden(2 * (b - 7) + 1)
                if b == 9:
                    gate_logits(0)
            for n in range(4, 8):
                gate_hidden(n)
            gate_logits(1)
            pe.wait_ge(p_const, 1)
            pe.wait_ge(v_sel, 1)
            pe.matmul(bank[0][:, 0:B * E], beforeb[:, :], selb[:, :, :], start=True, stop=True,
                      skip_group_check=True)
            for t in range(B - 1):
                mm = pe.matmul(bank[0][:, (t + 1) * E:B * E], onesb[:, :],
                               selb[:, t, :].unsqueeze(1).broadcast_to([128, B - 1 - t, E]), start=False,
                               stop=True, skip_group_check=True)
            mm.then_inc(t_pos, 1)
            for t in range(B):
                mm = pe.matmul(bank[1][:, 0:E], onesb[:, :], selb[:, t, :], start=(t == 0), stop=(t == B - 1))
            mm.then_inc(t_pos, 1)
            pe.wait_ge(l_ewi, 16)
            pe.wait_ge(l_ewo, 16)
            pe.wait_ge(v_wst, 1)
            pe.wait_ge(p_xs, B)
            nr = rounds(pe)
            with pe.Fori(0, nr) as r:
                for t in range(B):
                    pe.wait_ge(v_g, r * B + (t + 1))
                    g = GM[:, t, :, :].rearrange("p e j -> p (e j)")
                    for part in range(3):
                        mm = pe.matmul(bank[2][:, :], XS[:, part, t, :], g, start=(t == 0 and part == 0),
                                       stop=(t == B - 1 and part == 2))
                mm.then_inc(t_xg, 1)
                for t in range(B):
                    g = GM[:, t, :, :].rearrange("p e j -> p (e j)")
                    mm = pe.matmul(bank[0][0:24, :], wst[:, t, :, :].rearrange("p a e -> p (a e)"), g,
                                   start=(t == 0), stop=(t == B - 1))
                mm.then_inc(t_w24, 1)
                pe.wait_ge(a_xg, r + 1)
                for e in range(E):
                    for f in range(FT):
                        c = (e % 2) * 256 + f * J
                        mm = pe.matmul(bank[4 + e // 2][:, c:c + J], EWI[:, e, f * 128:f * 128 + 128],
                                       XG[:, e * J:e * J + J], start=True, stop=True)
                    if e % 2:
                        mm.then_inc(t_ez, 1)
                pe.wait_ge(a_w24, r + 1)
                for t in range(B):
                    if t >= 2:
                        pe.wait_ge(a_sm, r * B + (t - 1))
                    for p in range(NP):
                        mm = pe.transpose(bank[t % 2][:, 64 * p:64 * p + 64].bitcast(bf16),
                                          GM[:, t, 2 * p:2 * p + 2, :].rearrange("p e j -> p (e j)"), identb[:, :])
                    mm.then_inc(t_tr, 1)
                pe.wait_ge(a_sm, r * B + B)
                for p in range(NP):
                    mm = pe.matmul(bank[0][:, 24 * p:24 * p + 24], W24[:, 128 * p:128 * p + 128],
                                   pk("ident")[0:24, 0:24], start=True, stop=True)
                mm.then_inc(t_wt, 1)
                for e in range(E):
                    if e % 2 == 0:
                        pe.wait_ge(v_h, r * NP + (e // 2 + 1))
                    a, k = e % 2, e // 4
                    for f in range(FT):
                        mm = pe.matmul(bank[3 - k][J * a:J * a + J, 128 * (e // 2 % 2):128 * (e // 2 % 2) + 128],
                                       HE[:, e // 2, a, f, :], EWO[:, e, f, :], start=(f == 0), stop=(f == FT - 1))
                    if e % 4 == 3:
                        mm.then_inc(t_y, 1)
                for k in range(2):
                    pe.wait_ge(v_y, r * 4 + (2 * k + 2))
                    for t in range(B):
                        for p in range(2 * k, 2 * k + 2):
                            for part in range(3):
                                first = k == 0 and t % 4 == 0 and p == 0 and part == 0
                                mm = pe.matmul(bank[4 + t // 4][:, tok(t % 4)], SM[:, t, p, :], YS[:, part, p, :],
                                               start=first, stop=(p == NP - 1 and part == 2), skip_group_check=True)
                        if k == 1 and t % 4 == 3:
                            mm.then_inc(t_sc, 1)


def kernel(**inputs):
    import numpy as _np
    import concourse.bacc as _bacc
    from concourse import mybir as _mybir
    from concourse.bass_utils import run_bass_kernel_spmd as _run

    def arr(name):
        return _np.asarray(inputs[name])

    cols, width = pack_columns()
    pack = _np.zeros((128, width), _np.float32)

    def put(name, a):
        lo, hi = cols[name]
        pack[:a.shape[0], lo:hi] = a.reshape(a.shape[0], hi - lo)

    p = _np.arange(128)
    put("ident", _np.eye(128, dtype=_np.float32))
    put("before", _np.triu(_np.ones((128, 128), _np.float32), 1))
    slot = _np.where(p < 96, (p % 32) // 8, p % 4)
    put("slot_mask", (slot[:, None] == _np.arange(4)[None, :]).astype(_np.float32))
    put("iota_j", _np.broadcast_to(_np.arange(64, dtype=_np.float32), (128, 64)))
    put("iota_e", _np.broadcast_to(_np.arange(8, dtype=_np.float32), (128, 8)))
    own = _np.zeros((128, 4, 3, 8), _np.float32)
    for pair in range(4):
        own[p, pair, :, 2 * pair + p // 64] = 1.0
    put("own_e", own)

    put("wq", arr("L0_xattn_Wq").T)
    put("wk", arr("L0_xattn_Wk").T)
    put("wv", arr("L0_xattn_Wv").T)
    put("wo", arr("L0_xattn_Wo").T)
    put("bq", arr("L0_xattn_bq").reshape(128, 1))
    put("bk", arr("L0_xattn_bk").reshape(128, 1))
    for name, key in (("bv", "L0_xattn_bv"), ("bo", "L0_xattn_bo"), ("gbo", "L0_ffn_gate_bo")):
        put(name, _np.broadcast_to(arr(key), (128, 128)))
    put("gbi", arr("L0_ffn_gate_bi").reshape(4, 128).T)
    put("ebi", arr("L0_ffn_exp_bi").reshape(8, 4, 128).transpose(2, 0, 1))
    put("ebo", _np.repeat(arr("L0_ffn_exp_bo").reshape(4, 2, 128).transpose(1, 0, 2), 64, axis=0))

    c = _np.ascontiguousarray
    arrays = {
        "in_x": c(arr("x").transpose(1, 0, 2)),
        "in_ctxT": c(arr("ctx_1024").reshape(1024, 128).T),
        "in_mask": c(arr("mask_Bx1xSxS2_bk1").reshape(8, 128, 128).transpose(1, 0, 2)),
        "in_pack": pack,
        "in_gwi": c(arr("L0_ffn_gate_wi")),
        "in_gwo": c(arr("L0_ffn_gate_wo").reshape(4, 128, 128).transpose(1, 0, 2)),
        "in_ewi": c(arr("L0_ffn_exp_wi").transpose(1, 0, 2)),
        "in_ewo": c(arr("L0_ffn_exp_wo").reshape(8, 4, 128, 128).transpose(2, 0, 1, 3)),
    }
    nc = _bacc.Bacc("TRN2", target_bir_lowering=False, num_devices=1)
    args = [nc.dram_tensor(n, a.shape, _mybir.dt.from_np(a.dtype), kind="ExternalInput").ap() for n, a in arrays.items()]
    args.append(nc.dram_tensor("out_0", (128, 8, 128), _mybir.dt.float32, kind="ExternalOutput").ap())
    xattn_moe(nc, *args)
    r = _run(nc, [arrays], core_ids=[0])
    return c(r.results[0]["out_0"].transpose(1, 0, 2))
```

```python
import concourse.bass as bass
from concourse import mybir
from contextlib import ExitStack
import math


def pack_columns():
    widths = [("ident", 128), ("wk3", 384), ("wq3", 384), ("bk3", 4), ("bq3", 4), ("before", 128), ("slot_mask", 4), ("iota_j", 64), ("iota_e", 8),
              ("wq", 128), ("wk", 128), ("wv", 128), ("wo", 128), ("bq", 1), ("bk", 1),
              ("bv", 128), ("bo", 128), ("gbo", 128), ("gbi", 4), ("ebi", 32), ("ebo", 512), ("own_e", 96)]
    at, out = 0, {}
    for name, n in widths:
        out[name] = (at, at + n)
        at += n
    return out, at


def xattn_moe(nc, x, ctxT, mask, pack, gwi, gwo, ewi, ewo, out):
    f32, f32r, bf16, f16 = mybir.dt.float32, mybir.dt.float32r, mybir.dt.bfloat16, mybir.dt.float16
    i32, u32, u8 = mybir.dt.int32, mybir.dt.uint32, mybir.dt.uint8
    ALU, ACT, AX = mybir.AluOpType, mybir.ActivationFunctionType, mybir.AxisListType

    B, T, D = 8, 128, 128
    NG, NS, DH = 4, 4, 8
    F, E, J = 512, 8, 64
    FT = F // 128
    NP = E // 2
    KQ, KM = 96, 104
    BIG = float(2.0 ** 60)
    SCALE = 1.0 / math.sqrt(DH)
    EPS = 1e-5
    ALPHA, LAM = 1.6732632423543772848170429916717, 1.0507009873554804934193349852946
    PV = 27

    cols, _ = pack_columns()
    FIRST = cols["before"][0]

    ctx = ExitStack()
    with ctx:
        def sb(name, shape, dt=f32):
            return ctx.enter_context(nc.sbuf_tensor(name, shape, dt))

        def sem(name):
            return ctx.enter_context(nc.semaphore(name))

        X = sb("X", [128, B, D])
        EARLY = sb("EARLY", [128, 4 * B * T])
        CT = EARLY[:, 0:B * T]
        xnT = EARLY[:, 2 * B * T:3 * B * T]
        xn = EARLY[:, 3 * B * T:4 * B * T].rearrange("p (b d) -> p b d", b=B)
        HT = EARLY[:, :].rearrange("p (f n) -> p f n", f=FT)
        SM = EARLY[:, 0:2 * B * T].bitcast(bf16).rearrange("p (t a n) -> p t a n", t=B, a=NP)
        HE = EARLY[:, 2 * B * T:4 * B * T].rearrange("p (i a f j) -> p i a f j", i=NP, a=2, f=FT)
        PBUF = sb("PBUF", [128, 3072])
        PF = PBUF[:, 0:1024].rearrange("p (a n) -> p a n", a=2)
        PH = PBUF[:, 1024:2048].bitcast(f16).rearrange("p (a n) -> p a n", a=4)
        PL = PBUF[:, 2048:3072].bitcast(f16).rearrange("p (a n) -> p a n", a=4)
        GM = PBUF[:, 0:2048].bitcast(f16).rearrange("p (t e j) -> p t e j", t=B, e=E)
        ZB = PBUF[:, 2048:3072].rearrange("p (a n) -> p a n", a=2)
        MK = sb("MK", [128, B, T], u8)
        PK = sb("PK", list(pack.shape))
        GWI = sb("GWI", [128, F])
        GWO = sb("GWO", [128, FT, 128])
        EWI = sb("EWI", [128, E, F])
        EWO = sb("EWO", [128, E, FT, 128])

        def pk(name, rows=128):
            a, b = cols[name]
            return PK[0:rows, a:b]

        maskb = sb("maskb", [128, B, T], bf16)
        identb = sb("identb", [128, 128], bf16)
        identh = sb("identh", [128, 128], f16)
        negI = sb("negI", [128, 128], bf16)
        beforeb = sb("beforeb", [128, 128], bf16)
        onesb = sb("onesb", [128, 128], bf16)
        xb = sb("xb", [128, B, D])
        st1 = sb("st1", [128, B, 6])
        mv1 = sb("mv1", [128, B, 2])
        rs1 = sb("rs1", [128, B])
        HL = sb("HL", [128, 2, 2, 512], f32r)
        PAIR = sb("PAIR", [128, 2, 512])
        QR = sb("QR", [KM, NG, B * T], f32r)
        KR = sb("KR", [KM, NG, B * T], f32r)
        QX = sb("QX", [KM, 2, NS, NG, T], f32r)
        KX = sb("KX", [KQ, 2, NS, NG, T], f32r)
        VF = sb("VF", [128, 4, 16, DH])
        VT = sb("VT", [128, 4, 16, DH])
        VB = sb("VB", [128, B, 16, PV], bf16)
        NM = sb("NM", [128, 2, 16])
        MB = sb("MB", [128, 2, NG, 2, NS], bf16)
        UN = sb("UN", [128, 16, 9])
        RC = sb("RC", [128, 16])
        AT = sb("AT", [128, 2, 128])
        ATT = sb("ATT", [128, 2, 128])
        x1 = sb("x1", [128, B, D])
        st2 = sb("st2", [128, 2, 6])
        mv2 = sb("mv2", [128, 2, 2])
        rs2 = sb("rs2", [128, 2])
        xn2 = sb("xn2", [128, B, D])
        xn2T = sb("xn2T", [128, B * T])
        XS = sb("XS", [128, 2, B, D], f16)
        gb1 = sb("gb1", [128, FT])
        minus = sb("minus", [128, 128])
        ones1 = sb("ones1", [1, 128])
        gbo2 = sb("gbo2", [128, 128])
        lna = sb("lna", [128, 1])
        mhalf = sb("mhalf", [128, B])
        GE = sb("GE", [128, 2, 512])
        GR = PAIR
        top8 = sb("top8", [128, B, 8])
        idx8 = sb("idx8", [128, B, 8], u32)
        idxf = sb("idxf", [128, B, 2])
        tsum = sb("tsum", [128, B])
        rsum = sb("rsum", [128, B])
        tw = sb("tw", [128, B, 2])
        oh0 = sb("oh0", [128, B, E])
        oh1 = sb("oh1", [128, B, E])
        selb = sb("selb", [128, B, E], bf16)
        ww = sb("ww", [128, B, E])
        wr = sb("wr", [128, B, E])
        wst = sb("wst", [128, B, 3, E], bf16)
        pos = sb("pos", [128, B, E], f16)
        iota16 = sb("iota16", [128, J], f16)
        cmax = sb("cmax", [128, 1])
        nround = sb("nround", [128, 1], i32)
        XG = sb("XG", [128, E * J])
        EE = GE
        RR = GR
        WM = sb("WM", [128, NP, 24])
        wsl = sb("wsl", [128, NP])
        YF = PAIR[:, 0, :].rearrange("p (a d) -> p a d", a=NP)
        YR = PAIR[:, 1, :].rearrange("p (a d) -> p a d", a=NP)
        YS = sb("YS", [128, 3, NP, 128], bf16)
        fin = sb("fin", [1, 1])

        bank = [ctx.enter_context(nc.psum_tensor(f"bank{i}", [128, 512], f32)) for i in range(8)]

        l_first, l_pack, l_x, l_mask, l_gate, l_ewi, l_ewo, s_out = [
            sem(n) for n in ("l_first", "l_pack", "l_x", "l_mask", "l_gate", "l_ewi", "l_ewo", "s_out")]
        l_ctx = [sem(n) for n in ("l_ctx0", "l_ctx1")]
        l_kq = [sem(n) for n in ("l_k1", "l_q1")]
        l_kx = [sem(n) for n in ("l_kx0", "l_kx1")]
        p_ch, p_rs1, p_ident, p_const, p_xb, p_vb, p_pl, p_xs, p_rs2, p_wst = [
            sem(n) for n in ("p_ch", "p_rs1", "p_ident", "p_const", "p_xb", "p_vb", "p_pl", "p_xs", "p_rs2",
                             "p_wst")]
        v_ch, v_mv1, v_xn, v_mask, v_ld, v_lo, v_vf, v_kx, v_qx, v_max, v_mh, v_mb, v_un, v_rc, v_at = [
            sem(n) for n in ("v_ch", "v_mv1", "v_xn", "v_mask", "v_ld", "v_lo", "v_vf", "v_kx", "v_qx", "v_max", "v_mh",
                             "v_mb", "v_un", "v_rc", "v_at")]
        v_x1, v_st2, v_ag2, v_mv2, v_xn2, v_shift, v_ht, v_top, v_idx, v_sel, v_tw, v_n = [
            sem(n) for n in ("v_x1", "v_st2", "v_ag2", "v_mv2", "v_xn2", "v_shift", "v_ht", "v_top", "v_idx",
                             "v_sel", "v_tw", "v_n")]
        v_g, v_z, v_rr, v_h, v_w, v_yf, v_y, v_acc, v_fin = [
            sem(n) for n in ("v_g", "v_z", "v_rr", "v_h", "v_w", "v_yf", "v_y", "v_acc", "v_fin")]
        a_xnT, a_hd, a_hi, a_kx, a_qx, a_m, a_ph, a_pf, a_at, a_x2, a_xs, a_e, a_r, a_xg, a_ee, a_sm = [
            sem(n) for n in ("a_xnT", "a_hd", "a_hi", "a_kx", "a_qx", "a_m", "a_ph", "a_pf", "a_at", "a_x2", "a_xs", "a_e", "a_r", "a_xg",
                             "a_ee", "a_sm")]
        t_xn, t_v, t_dir, t_kq, t_s, t_m, t_st, t_pv, t_at, t_wo, t_x2, t_shift, t_z, t_lg, t_pos = [
            sem(n) for n in ("t_xn", "t_v", "t_dir", "t_kq", "t_s", "t_m", "t_st", "t_pv", "t_at", "t_wo", "t_x2", "t_shift", "t_z",
                             "t_lg", "t_pos")]
        t_xg, t_tr, t_ez, t_wt, t_y, t_sc = [
            sem(n) for n in ("t_xg", "t_tr", "t_ez", "t_wt", "t_y", "t_sc")]

        def tok(b, n=1):
            return slice(b * T, (b + n) * T)

        def logit_bank(t):
            return bank[(2, 3, 6, 7, 4, 5, 2, 3)[t]][:, 0:128]

        def rounds(eng):
            eng.wait_ge(v_n, 1)
            return eng.value_load(nround[0:1, 0:1], min_val=1, max_val=B * T // J)

        SPREAD = 3 * NG * 16
        LAST = B + 2
        NKA, KXB = 3, 5
        NQV = 3
        BLOCKS = 3 * NS * 16

        block = ctx.enter_context(nc.Block())

        @block.sync
        def _(sp):
            sp.dma_start(X[:, :, :], x).then_inc(l_x, 16)
            for h in range(2):
                sp.dma_start(CT[:, tok(4 * h, 4)], ctxT[:, tok(4 * h, 4)]).then_inc(l_ctx[h], 16)
            sp.dma_start(MK[:, :, :], mask).then_inc(l_mask, 16)

            for n, dst, parts in ((0, KR, (0, 0, 1)), (1, QR, (1, 0, 0))):
                sp.wait_ge(v_lo, n + 1)
                for row, part in enumerate(parts):
                    for g in range(NG):
                        sp.dma_start(dst[32 * row:32 * row + 32, g, tok(4, 4)].bitcast(f32),
                                     HL[32 * g:32 * g + 32, n, part, :].bitcast(f32)).then_inc(l_kq[n], 16)
            for b in range(KXB, B):
                sp.wait_ge(l_kq[0], SPREAD)
                sp.wait_ge(t_s, 4 * (b - 1))
                for part in range(3):
                    for s in range(NS):
                        rows = slice(32 * part + DH * s, 32 * part + DH * s + DH)
                        sp.dma_start(KX[rows, b % 2, s, :, :].bitcast(f32),
                                     KR[rows, :, tok(b)].bitcast(f32)).then_inc(l_kx[b % 2], 16)
            sp.dma_start(GWI[:, :], gwi).then_inc(l_gate, 16)
            sp.dma_start(GWO[:, :, :], gwo).then_inc(l_gate, 16)
            sp.dma_start(EWI[:, :, :], ewi).then_inc(l_ewi, 16)
            sp.dma_start(EWO[:, :, :, :], ewo).then_inc(l_ewo, 16)
            sp.wait_ge(v_fin, 1)
            sp.dma_start(out, x1[:, :, :]).then_inc(s_out, 16)
            sp.wait_ge(s_out, 16)

        @block.gpsimd
        def _(pool):
            chain = [0]

            def link(ins):
                chain[0] += 1
                ins.then_inc(p_ch, 1)
                pool.wait_ge(p_ch, chain[0])

            pool.memset(mhalf[:, :], -0.5)
            pool.memset(lna[:, :], math.log(ALPHA))
            link(pool.memset(onesb[:, :], 1.0))
            link(pool.memset(KR[KQ:KM, :, :].bitcast(f32), 1.0))
            for h in range(2):
                pool.wait_ge(v_mv1, h + 1)
                rs = rs1[:, 4 * h:4 * h + 4]
                pool.tensor_tensor(rs, rs, mhalf[:, 0:4], ALU.pow).then_inc(p_rs1, 1)
            pool.wait_ge(l_first, 16)
            pool.tensor_copy(identb[:, :], pk("ident"))
            pool.tensor_copy(identh[:, :], pk("ident"))
            pool.tensor_scalar(negI[:, :], pk("ident"), -BIG, None, ALU.mult).then_inc(p_ident, 1)
            link(pool.memset(VB[:, :, :, :], 0.0))
            link(pool.memset(VB[:, :, :, DH:DH + 1], 1.0))
            pool.wait_ge(l_pack, 16)
            pool.tensor_scalar(gb1[:, :], pk("gbi"), math.log(ALPHA), None, ALU.add)
            pool.memset(minus[:, :], -ALPHA)
            pool.memset(ones1[:, :], 1.0)
            pool.tensor_copy(beforeb[:, :], pk("before")).then_inc(p_const, 1)
            pool.tensor_tensor(xb[:, :, :], X[:, :, :], pk("bo").unsqueeze(1).broadcast_to([128, B, D]),
                               ALU.add).then_inc(p_xb, 1)
            for h in range(2):
                pool.wait_ge(v_vf, h + 1)
                vb = VB[:, 4 * h:4 * h + 4, :, :]
                link(pool.tensor_copy(vb[:, :, :, 0:DH], VF[:, :, :, :]))
                link(pool.tensor_tensor(VT[:, :, :, :], VF[:, :, :, :], vb[:, :, :, 0:DH], ALU.subtract))
                link(pool.tensor_copy(vb[:, :, :, 9:9 + DH], VT[:, :, :, :]))
                pool.tensor_tensor(vb[:, :, :, 18:18 + DH], VT[:, :, :, :], vb[:, :, :, 9:9 + DH],
                                   ALU.subtract).then_inc(p_vb, 1)
            for b in range(LAST + 1):
                for g in range(NG):
                    if g == NG - 1 and 0 <= b - 2 < B:
                        pool.wait_ge(v_mv2, b - 1)
                        pool.tensor_tensor(rs2[:, b % 2:b % 2 + 1], rs2[:, b % 2:b % 2 + 1], mhalf[:, 0:1],
                                           ALU.pow).then_inc(p_rs2, 1)
                    c = b - 3
                    if c >= 0 and g == 1:
                        pool.wait_ge(a_xs, c + 1)
                        pool.tensor_tensor(XS[:, 1, c, :], xn2[:, c, :], XS[:, 0, c, :], ALU.subtract).then_inc(p_xs, 1)
                    if b < B:
                        u = 4 * b + g
                        pool.wait_ge(a_pf, u + 1)
                        if b >= 1:
                            pool.wait_ge(t_pv, u - 3)
                        pool.tensor_tensor(PL[:, g, :], PF[:, u % 2, :], PH[:, g, :], ALU.subtract).then_inc(p_pl, 1)
            pool.wait_ge(v_tw, 1)
            pool.tensor_tensor(ww[:, :, :], oh0[:, :, :], tw[:, :, 0].unsqueeze(2).broadcast_to([128, B, E]), ALU.mult)
            link(pool.tensor_tensor(wr[:, :, :], oh1[:, :, :], tw[:, :, 1].unsqueeze(2).broadcast_to([128, B, E]),
                                    ALU.mult))
            link(pool.tensor_tensor(ww[:, :, :], ww[:, :, :], wr[:, :, :], ALU.add))
            link(pool.tensor_copy(wst[:, :, 0, :], ww[:, :, :]))
            link(pool.tensor_tensor(wr[:, :, :], ww[:, :, :], wst[:, :, 0, :], ALU.subtract))
            link(pool.tensor_copy(wst[:, :, 1, :], wr[:, :, :]))
            pool.tensor_tensor(wst[:, :, 2, :], wr[:, :, :], wst[:, :, 1, :], ALU.subtract).then_inc(p_wst, 1)

        @block.scalar
        def _(act):
            act.dma_start(PK[:, 0:FIRST], pack[:, 0:FIRST]).then_inc(l_first, 16)
            act.dma_start(PK[:, FIRST:], pack[:, FIRST:]).then_inc(l_pack, 16)

            def direct_high(n):
                g = n % NG
                act.wait_ge(t_dir, n + 1)
                act.activation((QR if n // NG else KR)[0:KQ, g, tok(0, 4)], bank[g][0:KQ, :], ACT.Identity,
                               bias=pk("bq3" if n // NG else "bk3", KQ)[:, g:g + 1]).then_inc(a_hd, 1)

            def high_part(n, name):
                act.wait_ge(t_kq, n + 1)
                act.activation(HL[:, n, 0, :], bank[5 + n][:, :], ACT.Identity, bias=pk(name)).then_inc(a_hi, 1)

            def turned_tokens(h):
                act.wait_ge(t_xn, h + 1)
                act.activation(xnT[:, tok(4 * h, 4)], bank[4][:, :], ACT.Copy).then_inc(a_xnT, 1)

            def max_rows(b):
                act.wait_ge(t_m, b + 1)
                act.activation(QR[KQ:KM, :, tok(b)], bank[6][KQ:KM, :].rearrange("p (g t) -> p g t", g=NG),
                               ACT.Copy).then_inc(a_m, 1)

            def expand_keys(b, s):
                if s == 0:
                    act.wait_ge(l_pack, 16)
                    if b >= 4:
                        act.wait_ge(l_kq[0], SPREAD)
                    else:
                        act.wait_ge(v_ld, NG)
                    if b >= 2:
                        act.wait_ge(t_s, 4 * (b - 1))
                act.activation(KX[:, b % 2, s, :, :], KR[0:KQ, :, tok(b)].bitcast(f32), ACT.Copy,
                               scale=pk("slot_mask", KQ)[:, s:s + 1]).then_inc(a_kx, 1)

            def expand_queries(b):
                if b >= 2:
                    act.wait_ge(t_st, 4 * (b - 1))
                act.wait_ge(a_m, b + 1)
                if b >= 4:
                    act.wait_ge(l_kq[1], SPREAD)
                else:
                    act.wait_ge(v_ld, 2 * NG)
                for s in range(NQV, NS):
                    act.activation(QX[:, b % 2, s, :, :], QR[:, :, tok(b)].bitcast(f32), ACT.Copy,
                                   scale=pk("slot_mask", KM)[:, s:s + 1]).then_inc(a_qx, 1)

            def gate_exp(n):
                act.wait_ge(t_z, n + 1)
                if n >= 2:
                    act.wait_ge(v_ht, n - 1)
                act.activation(GE[:, n % 2, :], bank[n % 2][:, :], ACT.Exp,
                               bias=gb1[:, n % FT:n % FT + 1]).then_inc(a_e, 1)
                act.activation(GR[:, n % 2, :], bank[n % 2][:, :], ACT.Relu,
                               bias=pk("gbi")[:, n % FT:n % FT + 1]).then_inc(a_r, 1)

            for n in range(NG):
                direct_high(n)
            turned_tokens(0)
            for s in range(NKA):
                expand_keys(0, s)
            for n in range(NG, 2 * NG):
                direct_high(n)
            turned_tokens(1)
            for s in range(NKA):
                expand_keys(1, s)
            high_part(0, "bk")
            high_part(1, "bq")
            for s in range(NKA):
                expand_keys(2, s)
            max_rows(0)
            expand_queries(0)
            for b in range(LAST + 1):
                if b + 1 < B:
                    max_rows(b + 1)
                for g in range(NG):
                    if b < B:
                        u = 4 * b + g
                        act.wait_ge(t_st, u + 1)
                        if b >= 1:
                            act.wait_ge(t_pv, u - 3)
                        act.activation(PH[:, g, :], bank[2 + u % 2][:, :], ACT.Exp, scale=SCALE).then_inc(a_ph, 1)
                        if u >= 2:
                            act.wait_ge(p_pl, u - 1)
                        act.activation(PF[:, u % 2, :], bank[2 + u % 2][:, :], ACT.Exp, scale=SCALE).then_inc(a_pf, 1)
                    if g == 0 and b + 1 < B:
                        expand_queries(b + 1)
                    if b + 3 < KXB and g < NKA:
                        expand_keys(b + 3, g)
                    c = b - 3
                    if g == 0 and 0 <= b - 2 < B:
                        act.wait_ge(t_at, b - 2 + 1)
                        act.activation(ATT[:, b % 2, :], bank[4][:, 0:128], ACT.Copy).then_inc(a_at, 1)
                    if g == 0 and c >= 0:
                        act.wait_ge(v_xn2, c + 1)
                        act.activation(XS[:, 0, c, :], xn2[:, c, :], ACT.Copy).then_inc(a_xs, 1)
                    if g == 2 and c >= 0:
                        act.wait_ge(t_x2, c + 1)
                        act.activation(xn2T[:, tok(c)], bank[5][:, tok(c % 4)], ACT.Copy).then_inc(a_x2, 1)
                    if (b, g) == (B - 1, NG - 1):
                        act.wait_ge(p_const, 1)
                        gate_exp(0)
                    if (b, g) == (B, 0):
                        gate_exp(1)
                    if (b, g) == (B, NG - 1):
                        gate_exp(2)
                    if (b, g) == (B + 1, 1):
                        gate_exp(3)
            for n in range(4, 8):
                gate_exp(n)
            nr = rounds(act)
            with act.Fori(0, nr) as r:
                act.wait_ge(t_xg, r + 1)
                act.activation(XG[:, :], bank[2][:, :], ACT.Copy).then_inc(a_xg, 1)

                def exponential(i):
                    act.wait_ge(v_z, r * NP + (i + 1))
                    if i >= 2:
                        act.wait_ge(v_h, r * NP + (i - 1))
                    act.activation(EE[:, i % 2, :], ZB[:, i % 2, :], ACT.Exp, bias=lna[:, :]).then_inc(a_ee, 1)

                def scatter_matrix(t):
                    act.wait_ge(t_tr, r * B + (t + 1))
                    act.activation(SM[:, t, :, :], bank[t % 2][:, 0:256].bitcast(f16).rearrange(
                        "p (a n) -> p a n", a=NP), ACT.Copy).then_inc(a_sm, 1)

                for i in range(NP):
                    exponential(i)
                    scatter_matrix(i)
                for t in range(NP, B):
                    scatter_matrix(t)

        @block.vector
        def _(dve):
            chain = [0]

            def link(ins):
                chain[0] += 1
                ins.then_inc(v_ch, 1)
                dve.wait_ge(v_ch, chain[0])

            dve.wait_ge(l_x, 16)
            for h in range(2):
                for b in range(4 * h, 4 * h + 4):
                    ins = dve.bn_stats(st1[:, b, :], X[:, b, :])
                link(ins)
                for b in range(4 * h, 4 * h + 4):
                    ins = dve.bn_aggr(mv1[:, b, :], st1[:, b, :])
                link(ins)
                dve.tensor_scalar(rs1[:, 4 * h:4 * h + 4], mv1[:, 4 * h:4 * h + 4, 1], EPS, None,
                                  ALU.add).then_inc(v_mv1, 1)
            for h in range(2):
                dve.wait_ge(p_rs1, h + 1)
                for b in range(4 * h, 4 * h + 4):
                    dve.tensor_scalar(xn[:, b, :], X[:, b, :], mv1[:, b, 0:1], rs1[:, b:b + 1], ALU.subtract,
                                      ALU.mult).then_inc(v_xn, 1)
            def direct_low(n):
                g, dst, bias = n % NG, (QR if n // NG else KR), pk("bq3" if n // NG else "bk3")
                rows = slice(0, 32) if n // NG else slice(64, 96)
                dve.wait_ge(a_hd, n + 1)
                dve.scalar_tensor_tensor(out=dst[rows, g, tok(0, 4)], in0=bank[g][rows, :], scalar=bias[rows, g:g + 1],
                                         in1=dst[rows, g, tok(0, 4)], op0=ALU.add, op1=ALU.subtract).then_inc(v_ld, 1)

            def low_part(n, name):
                dve.wait_ge(a_hi, n + 1)
                dve.scalar_tensor_tensor(out=HL[:, n, 1, :], in0=bank[5 + n][:, :], scalar=pk(name),
                                         in1=HL[:, n, 0, :], op0=ALU.add, op1=ALU.subtract).then_inc(v_lo, 1)

            def biased_values(h):
                dve.wait_ge(t_v, h + 1)
                if h == 1:
                    dve.wait_ge(p_vb, 1)
                dve.tensor_tensor(VF[:, :, :, :].rearrange("p b h d -> p b (h d)"),
                                  bank[7][:, :].rearrange("p (b d) -> p b d", b=4),
                                  pk("bv").unsqueeze(1).broadcast_to([128, 4, 128]), ALU.add).then_inc(v_vf, 1)


            def expand_keys(b):
                dve.wait_ge(l_pack, 16)
                if b >= 4:
                    dve.wait_ge(l_kq[0], SPREAD)
                else:
                    dve.wait_ge(v_ld, NG)
                if b >= 2:
                    dve.wait_ge(t_s, 4 * (b - 1))
                for s in range(NKA, NS):
                    dve.tensor_scalar(KX[:, b % 2, s, :, :], KR[0:KQ, :, tok(b)].bitcast(f32),
                                      pk("slot_mask", KQ)[:, s:s + 1], None, ALU.mult).then_inc(v_kx, 1)

            def expand_queries(b, slots):
                if slots[0] == 0:
                    dve.wait_ge(a_m, b + 1)
                    if b >= 4:
                        dve.wait_ge(l_kq[1], SPREAD)
                    else:
                        dve.wait_ge(v_ld, 2 * NG)
                    if b >= 2:
                        dve.wait_ge(t_st, 4 * (b - 1))
                for s in slots:
                    dve.tensor_scalar(QX[:, b % 2, s, :, :], QR[:, :, tok(b)].bitcast(f32),
                                      pk("slot_mask", KM)[:, s:s + 1], None, ALU.mult).then_inc(v_qx, 1)

            def row_max(b, g):
                u = 4 * b + g
                dve.wait_ge(t_s, u + 1)
                dve.tensor_reduce(NM[:, b % 2, NS * g:NS * g + NS],
                                  bank[u % 2][:, :].rearrange("p (s k) -> p s k", s=NS), AX.X, ALU.max,
                                  negate=True).then_inc(v_max, 1)

            def split_max(b, part):
                nm = NM[:, b % 2, :].rearrange("p (g s) -> p g s", g=NG)
                if part == 0:
                    dve.wait_ge(v_max, 4 * b + 4)
                    if b >= 2:
                        dve.wait_ge(t_m, b - 1)
                    dve.tensor_copy(MB[:, b % 2, :, 0, :], nm).then_inc(v_mh, 1)
                else:
                    dve.wait_ge(v_mh, b + 1)
                    dve.tensor_tensor(MB[:, b % 2, :, 1, :], nm, MB[:, b % 2, :, 0, :], ALU.subtract).then_inc(v_mb, 1)

            def normalise(b, step):
                if step == 0:
                    dve.wait_ge(t_pv, 4 * b + 4)
                    if b >= 1:
                        dve.wait_ge(v_at, b)
                    dve.tensor_reduce(UN[:, :, :], bank[7][:, 0:16 * PV].rearrange("p (h a c) -> p h c a", h=16, a=3),
                                      AX.X, ALU.add).then_inc(v_un, 1)
                if step == 1:
                    dve.wait_ge(v_un, b + 1)
                    dve.reciprocal(RC[:, :], UN[:, :, DH]).then_inc(v_rc, 1)
                if step == 2:
                    dve.wait_ge(v_rc, b + 1)
                    dve.tensor_tensor(AT[:, b % 2, :].rearrange("p (h d) -> p h d", h=16), UN[:, :, 0:DH],
                                      RC[:, :].unsqueeze(2).broadcast_to([128, 16, DH]), ALU.mult).then_inc(v_at, 1)

            def second_norm(b, step):
                c = b % 2
                if step == 0:
                    dve.wait_ge(t_wo, b + 1)
                    if b == 0:
                        dve.wait_ge(p_xb, 1)
                    dve.tensor_tensor(x1[:, b, :], bank[4][:, 128:256], xb[:, b, :], ALU.add).then_inc(v_x1, 1)
                if step == 1:
                    dve.wait_ge(v_x1, b + 1)
                    dve.bn_stats(st2[:, c, :], x1[:, b, :]).then_inc(v_st2, 1)
                if step == 2:
                    dve.wait_ge(v_st2, b + 1)
                    dve.bn_aggr(mv2[:, c, :], st2[:, c, :]).then_inc(v_ag2, 1)
                if step == 3:
                    dve.wait_ge(v_ag2, b + 1)
                    dve.tensor_scalar(rs2[:, c:c + 1], mv2[:, c, 1:2], EPS, None, ALU.add).then_inc(v_mv2, 1)
                if step == 4:
                    dve.wait_ge(p_rs2, b + 1)
                    dve.tensor_scalar(xn2[:, b, :], x1[:, b, :], mv2[:, c, 0:1], rs2[:, c:c + 1], ALU.subtract,
                                      ALU.mult).then_inc(v_xn2, 1)

            def gate_shift():
                dve.wait_ge(t_shift, 1)
                dve.scalar_tensor_tensor(out=gbo2[:, :], in0=pk("gbo"), scalar=1.0 / LAM, in1=bank[0][:, 0:128],
                                         op0=ALU.mult, op1=ALU.add).then_inc(v_shift, 1)

            def gate_selu(n):
                dve.wait_ge(a_e, n + 1)
                dve.wait_ge(a_r, n + 1)
                dve.scalar_tensor_tensor(out=HT[:, n % FT, tok(4 * (n // FT), 4)], in0=GE[:, n % 2, :], scalar=ALPHA,
                                         in1=GR[:, n % 2, :], op0=ALU.min, op1=ALU.add).then_inc(v_ht, 1)

            def gate_max(t):
                dve.wait_ge(t_lg, t + 1)
                dve.max(top8[:, t, :], logit_bank(t)).then_inc(v_top, 1)

            def gate_index(t):
                dve.wait_ge(v_top, t + 1)
                dve.max_index(idx8[:, t, :], top8[:, t, :], logit_bank(t)).then_inc(v_idx, 1)

            dve.wait_ge(l_pack, 16)
            dve.tensor_scalar(iota16[:, :], pk("iota_j"), 1.0, None, ALU.add)
            dve.wait_ge(l_mask, 16)
            dve.tensor_copy(maskb[:, :, :], MK[:, :, :]).then_inc(v_mask, 1)
            for n in range(NG):
                direct_low(n)
            expand_keys(0)
            biased_values(0)
            for n in range(NG, 2 * NG):
                direct_low(n)
            expand_keys(1)
            row_max(0, 0)
            row_max(0, 1)
            low_part(0, "bk")
            row_max(0, 2)
            low_part(1, "bq")
            row_max(0, 3)
            split_max(0, 0)
            split_max(0, 1)
            biased_values(1)
            row_max(1, 0)
            row_max(1, 1)
            expand_queries(0, (0, 1))
            row_max(1, 2)
            expand_queries(0, (2,))
            row_max(1, 3)
            split_max(1, 0)
            split_max(1, 1)
            expand_keys(2)
            for b in range(B - 1):
                if b + 2 < B:
                    row_max(b + 2, 0)
                if b >= 3:
                    second_norm(b - 3, 4)
                if b + 1 < B:
                    expand_queries(b + 1, (0, 1))
                if b + 2 < B:
                    row_max(b + 2, 1)
                if b + 1 < B:
                    expand_queries(b + 1, (2,))
                if b + 2 < B:
                    row_max(b + 2, 2)
                if b >= 2:
                    second_norm(b - 2, 0)
                if b + 3 < KXB:
                    expand_keys(b + 3)
                if b >= 2:
                    second_norm(b - 2, 1)
                if b + 2 < B:
                    row_max(b + 2, 3)
                if b >= 2:
                    second_norm(b - 2, 2)
                if b + 2 < B:
                    split_max(b + 2, 0)
                if b >= 2:
                    second_norm(b - 2, 3)
                if b + 2 < B:
                    split_max(b + 2, 1)
                if b >= 1:
                    for step in range(3):
                        normalise(b - 1, step)
            second_norm(B - 4, 4)
            gate_shift()
            for step in range(4):
                second_norm(B - 3, step)
            for step in range(3):
                normalise(B - 2, step)
            second_norm(B - 3, 4)
            gate_selu(0)
            second_norm(B - 2, 0)
            second_norm(B - 2, 1)
            for step in range(3):
                normalise(B - 1, step)
            second_norm(B - 2, 2)
            second_norm(B - 2, 3)
            gate_selu(1)
            second_norm(B - 2, 4)
            second_norm(B - 1, 0)
            second_norm(B - 1, 1)
            gate_selu(2)
            second_norm(B - 1, 2)
            second_norm(B - 1, 3)
            gate_selu(3)
            second_norm(B - 1, 4)
            gate_selu(4)
            gate_selu(5)
            for t in range(2):
                gate_max(t)
                gate_index(t)
            gate_selu(6)
            for t in range(2, 4):
                gate_max(t)
                gate_index(t)
            gate_selu(7)
            gate_max(4)
            for t in range(5, 8):
                gate_max(t)
                gate_index(t - 1)
            gate_index(7)
            dve.wait_ge(v_idx, B)

            def each(ap):
                return ap.unsqueeze(2).broadcast_to([128, B, E])

            dve.tensor_tensor(tsum[:, :], top8[:, :, 0], top8[:, :, 1], ALU.add)
            link(dve.tensor_copy(idxf[:, :, :], idx8[:, :, 0:2]))
            iota_e = pk("iota_e").unsqueeze(1).broadcast_to([128, B, E])
            dve.tensor_tensor(oh0[:, :, :], iota_e, each(idxf[:, :, 0]), ALU.is_equal)
            link(dve.tensor_tensor(oh1[:, :, :], iota_e, each(idxf[:, :, 1]), ALU.is_equal))
            dve.tensor_tensor(selb[:, :, :], oh0[:, :, :], oh1[:, :, :], ALU.add).then_inc(v_sel, 1)
            link(dve.reciprocal(rsum[:, :], tsum[:, :]))
            dve.tensor_tensor(tw[:, :, :], top8[:, :, 0:2], rsum[:, :].unsqueeze(2).broadcast_to([128, B, 2]),
                              ALU.mult).then_inc(v_tw, 1)
            dve.wait_ge(t_pos, 2)
            link(dve.tensor_reduce(cmax[:, :], bank[1][:, 0:E], AX.X, ALU.max))
            link(dve.tensor_scalar(cmax[:, :], cmax[:, :], 1.0 / J, (J - 1) / (2.0 * J), ALU.mult, ALU.add))
            dve.tensor_scalar(nround[:, :], cmax[:, :], 1.0, None, ALU.max).then_inc(v_n, 1)
            link(dve.scalar_tensor_tensor(out=pos[:, :, :], in0=bank[0][:, 0:B * E].rearrange("p (t e) -> p t e", t=B),
                                          scalar=1.0, in1=selb[:, :, :], op0=ALU.add, op1=ALU.mult))
            nr = rounds(dve)
            with dve.Fori(0, nr) as r:
                for t in range(B):
                    dve.tensor_tensor(GM[:, t, :, :], pos[:, t, :].unsqueeze(2).broadcast_to([128, E, J]),
                                      iota16[:, :].unsqueeze(1).broadcast_to([128, E, J]),
                                      ALU.is_equal).then_inc(v_g, 1)
                dve.wait_ge(v_g, r * B + B)
                dve.tensor_scalar(pos[:, :, :], pos[:, :, :], -float(J), None, ALU.add).then_inc(v_w, 1)

                def biased(i):
                    dve.wait_ge(t_ez, r * NP + (i + 1))
                    if i >= 2:
                        dve.wait_ge(a_ee, r * NP + (i - 1))
                        dve.wait_ge(v_rr, r * NP + (i - 1))
                    dve.tensor_tensor(ZB[:, i % 2, :].rearrange("p (c j) -> p c j", j=J),
                                      bank[4 + i][:, :].rearrange("p (c j) -> p c j", j=J),
                                      pk("ebi")[:, 8 * i:8 * i + 8].unsqueeze(2).broadcast_to([128, 8, J]),
                                      ALU.add).then_inc(v_z, 1)

                def selu_low(i):
                    dve.wait_ge(v_z, r * NP + (i + 1))
                    if i >= 2:
                        dve.wait_ge(v_h, r * NP + (i - 1))
                    dve.tensor_scalar(RR[:, i % 2, :], ZB[:, i % 2, :], -ALPHA, -ALPHA, ALU.add,
                                      ALU.max).then_inc(v_rr, 1)

                def selu_sum(i):
                    dve.wait_ge(a_ee, r * NP + (i + 1))
                    dve.wait_ge(v_rr, r * NP + (i + 1))
                    dve.scalar_tensor_tensor(out=HE[:, i, :, :, :].rearrange("p a f j -> p (a f j)"),
                                             in0=EE[:, i % 2, :], scalar=ALPHA, in1=RR[:, i % 2, :], op0=ALU.min,
                                             op1=ALU.add).then_inc(v_h, 1)

                biased(0)
                selu_low(0)
                dve.wait_ge(t_wt, r + 1)
                dve.tensor_tensor(WM[:, :, :], bank[1][:, 0:96].rearrange("p (a c) -> p a c", a=NP),
                                  pk("own_e").rearrange("p (a c) -> p a c", a=NP), ALU.mult).then_inc(v_w, 1)
                biased(1)
                selu_sum(0)
                selu_low(1)
                biased(2)
                selu_sum(1)
                selu_low(2)
                biased(3)
                dve.wait_ge(v_w, r * 3 + 2)
                dve.tensor_reduce(wsl[:, :], WM[:, :, :], AX.X, ALU.add).then_inc(v_w, 1)
                selu_sum(2)
                selu_low(3)
                selu_sum(3)
                for k in range(2):
                    dve.wait_ge(t_y, r * 2 + (k + 1))
                    dve.scalar_tensor_tensor(out=YF[:, 2 * k:2 * k + 2, :],
                                             in0=bank[3 - k][:, 0:256].rearrange("p (a d) -> p a d", a=2), scalar=LAM,
                                             in1=pk("ebo").rearrange("p (a d) -> p a d", a=NP)[:, 2 * k:2 * k + 2, :],
                                             op0=ALU.mult, op1=ALU.add).then_inc(v_yf, 1)
                    dve.wait_ge(v_yf, r * 8 + (4 * k + 1))
                    dve.wait_ge(v_w, r * 3 + 3)
                    dve.tensor_tensor(YF[:, 2 * k:2 * k + 2, :], YF[:, 2 * k:2 * k + 2, :],
                                      wsl[:, 2 * k:2 * k + 2].unsqueeze(2).broadcast_to([128, 2, 128]),
                                      ALU.mult).then_inc(v_yf, 1)
                    dve.wait_ge(v_yf, r * 8 + (4 * k + 2))
                    dve.tensor_copy(YS[:, 0, 2 * k:2 * k + 2, :], YF[:, 2 * k:2 * k + 2, :]).then_inc(v_y, 1)
                    dve.wait_ge(v_y, r * 4 + (2 * k + 1))
                    dve.tensor_tensor(YR[:, 2 * k:2 * k + 2, :], YF[:, 2 * k:2 * k + 2, :],
                                      YS[:, 0, 2 * k:2 * k + 2, :], ALU.subtract).then_inc(v_yf, 1)
                    dve.wait_ge(v_yf, r * 8 + (4 * k + 3))
                    dve.tensor_copy(YS[:, 1, 2 * k:2 * k + 2, :], YR[:, 2 * k:2 * k + 2, :]).then_inc(v_yf, 1)
                    dve.wait_ge(v_yf, r * 8 + (4 * k + 4))
                    dve.tensor_tensor(YS[:, 2, 2 * k:2 * k + 2, :], YR[:, 2 * k:2 * k + 2, :],
                                      YS[:, 1, 2 * k:2 * k + 2, :], ALU.subtract).then_inc(v_y, 1)
                for k in range(2):
                    dve.wait_ge(t_sc, r * 2 + (k + 1))
                    dve.tensor_tensor(x1[:, 4 * k:4 * k + 4, :],
                                      bank[4 + k][:, :].rearrange("p (t d) -> p t d", t=4),
                                      x1[:, 4 * k:4 * k + 4, :], ALU.add).then_inc(v_acc, 1)
                dve.wait_ge(v_acc, r * 2 + 2)
            dve.memset(fin[:, :], 0.0).then_inc(v_fin, 1)

        @block.tensor
        def _(pe):
            def direct(n):
                g = n % NG
                if n == NG:
                    pe.wait_ge(a_xnT, 1)
                if n >= NG:
                    pe.wait_ge(v_ld, n - NG + 1)
                pe.matmul(bank[g][0:KQ, :], pk("wq3" if n // NG else "wk3")[:, KQ * g:KQ * g + KQ],
                          (xnT if n // NG else CT)[:, tok(0, 4)], start=True, stop=True).then_inc(t_dir, 1)

            def project(n):
                if n:
                    pe.wait_ge(a_xnT, 2)
                pe.matmul(bank[5 + n][:, :], pk("wq" if n else "wk"), (xnT if n else CT)[:, tok(4, 4)],
                          start=True, stop=True).then_inc(t_kq, 1)

            def turn_tokens(h):
                pe.wait_ge(v_xn, 4 * h + 4)
                for b in range(4):
                    mm = pe.transpose(bank[4][:, tok(b)], xn[:, 4 * h + b, :], pk("ident"))
                mm.then_inc(t_xn, 1)

            def values_in(h):
                if h == 1:
                    pe.wait_ge(v_vf, 1)
                for b in range(4):
                    mm = pe.matmul(bank[7][:, tok(b)], CT[:, tok(4 * h + b)], pk("wv"), start=True, stop=True)
                mm.then_inc(t_v, 1)

            pe.wait_ge(l_first, 16)
            pe.wait_ge(l_ctx[0], 16)
            for n in range(NG):
                direct(n)
            turn_tokens(0)
            pe.wait_ge(l_pack, 16)
            values_in(0)
            for n in range(NG, 2 * NG):
                direct(n)
            turn_tokens(1)
            pe.wait_ge(l_ctx[1], 16)
            pe.wait_ge(p_ident, 1)
            pe.wait_ge(v_mask, 1)

            def scores(b, g):
                u = 4 * b + g
                if u >= 2:
                    pe.wait_ge(v_max, u - 1)
                pe.matmul(bank[u % 2][:, :], negI[:, :], maskb[:, b, :].unsqueeze(1).broadcast_to([128, NS, T]),
                          start=True, stop=False)
                if g == 0:
                    if b < KXB:
                        pe.wait_ge(a_kx, NKA * (b + 1))
                        pe.wait_ge(v_kx, (NS - NKA) * (b + 1))
                    else:
                        pe.wait_ge(l_kx[b % 2], BLOCKS * ((b - KXB) // 2 + 1))
                    if b >= 4:
                        pe.wait_ge(l_kq[1], SPREAD)
                pe.matmul(bank[u % 2][:, :], QR[0:KQ, g, tok(b)], KX[:, b % 2, :, g, :], start=False,
                          stop=True).then_inc(t_s, 1)

            def turned_scores(b, g):
                u = 4 * b + g
                if u >= 2:
                    pe.wait_ge(a_pf, u - 1)
                pe.matmul(bank[2 + u % 2][:, :], maskb[:, b, :], negI[:, :].unsqueeze(1).broadcast_to([128, NS, T]),
                          start=True, stop=False)
                if g == 0:
                    pe.wait_ge(v_qx, NQV * (b + 1))
                    pe.wait_ge(a_qx, (NS - NQV) * (b + 1))
                pe.matmul(bank[2 + u % 2][:, :], KR[:, g, tok(b)], QX[:, b % 2, :, g, :], start=False,
                          stop=True).then_inc(t_st, 1)

            def turn_max(b):
                pe.wait_ge(v_mb, b + 1)
                if b >= 1:
                    pe.wait_ge(a_m, b)
                else:
                    pe.wait_ge(v_lo, 2)
                for g in range(NG):
                    mm = pe.matmul(bank[6][KQ:KM, tok(g)], MB[:, b % 2, g, :, :].rearrange("p a s -> p (a s)"),
                                   identb[:, :], start=True, stop=True)
                mm.then_inc(t_m, 1)

            def values(b, g):
                u = 4 * b + g
                pe.wait_ge(p_pl, u + 1)
                if g == 0:
                    pe.wait_ge(p_vb, b // 4 + 1)
                    if b >= 1:
                        pe.wait_ge(v_un, b)
                for s in range(NS):
                    h = NS * g + s
                    o = bank[7][:, h * PV:h * PV + PV]
                    pe.matmul(o, PH[:, g, tok(s)], VB[:, b, h, :], start=True, stop=False)
                    mm = pe.matmul(o, PL[:, g, tok(s)], VB[:, b, h, :], start=False, stop=True)
                mm.then_inc(t_pv, 1)

            def gate_hidden(n):
                h, f = n // FT, n % FT
                if f == 0:
                    pe.wait_ge(a_x2, 4 * h + 4)
                if n >= 2:
                    pe.wait_ge(a_r, n - 1)
                elif n == 0:
                    pe.wait_ge(v_shift, 1)
                pe.matmul(bank[n % 2][:, :], GWI[:, f * 128:f * 128 + 128], xn2T[:, tok(4 * h, 4)], start=True,
                          stop=True).then_inc(t_z, 1)

            def gate_shift():
                for f in range(FT):
                    mm = pe.matmul(bank[0][:, 0:128], minus[:, :], GWO[:, f, :], start=(f == 0), stop=(f == FT - 1))
                mm.then_inc(t_shift, 1)

            def gate_bias(t):
                if t == 0:
                    pe.wait_ge(a_pf, 4 * B)
                    pe.wait_ge(a_m, B)
                elif t == 3:
                    pe.wait_ge(v_un, B)
                elif t == 4:
                    pe.wait_ge(v_x1, B)
                elif t > 5:
                    pe.wait_ge(v_idx, t - 5)
                pe.matmul(logit_bank(t), ones1[:, :], gbo2[0:1, :], start=True, stop=False)

            def gate_logits(h, f):
                pe.wait_ge(v_ht, FT * h + f + 1)
                for t in range(4 * h, 4 * h + 4):
                    mm = pe.matmul(logit_bank(t), HT[:, f, tok(t)], GWO[:, f, :], start=False, stop=(f == FT - 1))
                    if f == FT - 1:
                        mm.then_inc(t_lg, 1)

            pe.wait_ge(v_ld, 2 * NG)
            scores(0, 0)
            scores(0, 1)
            project(0)
            scores(0, 2)
            project(1)
            scores(0, 3)
            values_in(1)
            scores(1, 0)
            turn_max(0)
            for g in range(1, NG):
                scores(1, g)
            for b in range(LAST + 1):
                if b + 1 < B:
                    turn_max(b + 1)
                for g in range(NG):
                    if b < B:
                        turned_scores(b, g)
                    if b + 2 < B:
                        scores(b + 2, g)
                    if 0 <= b - 1 < B:
                        values(b - 1, g)
                    if g == 0 and 0 <= b - 2 < B:
                        pe.wait_ge(v_at, b - 2 + 1)
                        if b >= 3:
                            pe.wait_ge(v_x1, b - 2)
                        pe.transpose(bank[4][:, 0:128], AT[:, b % 2, :], pk("ident")).then_inc(t_at, 1)
                    if (b, g) == (B + 1, 1):
                        for t in range(4):
                            gate_bias(t)
                    if g == 1 and 0 <= b - 2 < B:
                        pe.wait_ge(a_at, b - 2 + 1)
                        pe.matmul(bank[4][:, 128:256], ATT[:, b % 2, :], pk("wo"), start=True,
                                  stop=True).then_inc(t_wo, 1)
                    if g == 2 and 0 <= b - 3 < B:
                        pe.wait_ge(v_xn2, b - 3 + 1)
                        if b - 3 >= 1:
                            pe.wait_ge(a_x2, b - 3)
                        pe.transpose(bank[5][:, tok((b - 3) % 4)], xn2[:, b - 3, :], pk("ident")).then_inc(t_x2, 1)
                if b == B - 2:
                    pe.wait_ge(l_gate, 32)
                    pe.wait_ge(v_max, 4 * B)
                    pe.wait_ge(p_const, 1)
                    gate_shift()
                if b == B + 1:
                    for f in range(3):
                        gate_logits(0, f)
                if b in (B - 1, B):
                    gate_hidden(2 * (b - B + 1))
                    gate_hidden(2 * (b - B + 1) + 1)
            gate_hidden(4)
            gate_hidden(5)
            gate_logits(0, 3)
            gate_hidden(6)
            gate_bias(4)
            gate_bias(5)
            gate_hidden(7)
            gate_bias(6)
            gate_bias(7)
            for f in range(FT):
                gate_logits(1, f)
            pe.wait_ge(p_const, 1)
            pe.wait_ge(v_sel, 1)
            pe.matmul(bank[0][:, 0:B * E], beforeb[:, :], selb[:, :, :], start=True, stop=True,
                      skip_group_check=True)
            for t in range(B - 1):
                mm = pe.matmul(bank[0][:, (t + 1) * E:B * E], onesb[:, :],
                               selb[:, t, :].unsqueeze(1).broadcast_to([128, B - 1 - t, E]), start=False,
                               stop=True, skip_group_check=True)
            mm.then_inc(t_pos, 1)
            for t in range(B):
                mm = pe.matmul(bank[1][:, 0:E], onesb[:, :], selb[:, t, :], start=(t == 0), stop=(t == B - 1))
            mm.then_inc(t_pos, 1)
            pe.wait_ge(l_ewi, 16)
            pe.wait_ge(l_ewo, 16)
            pe.wait_ge(p_xs, B)
            nr = rounds(pe)
            with pe.Fori(0, nr) as r:
                for t in range(B):
                    pe.wait_ge(v_g, r * B + (t + 1))
                    g = GM[:, t, :, :].rearrange("p e j -> p (e j)")
                    for part in range(2):
                        mm = pe.matmul(bank[2][:, :], XS[:, part, t, :], g, start=(t == 0 and part == 0),
                                       stop=(t == B - 1 and part == 1))
                mm.then_inc(t_xg, 1)
                pe.wait_ge(p_wst, 1)
                for p in range(NP):
                    for t in range(B):
                        mm = pe.matmul(bank[1][:, 24 * p:24 * p + 24],
                                       GM[:, t, 2 * p:2 * p + 2, :].rearrange("p e j -> p (e j)"),
                                       wst[:, t, :, :].rearrange("p a e -> p (a e)"), start=(t == 0), stop=(t == B - 1))
                mm.then_inc(t_wt, 1)
                pe.wait_ge(a_xg, r + 1)
                def expert_in(i):
                    for e in (2 * i, 2 * i + 1):
                        for f in range(FT):
                            c = (e % 2) * 256 + f * J
                            mm = pe.matmul(bank[4 + i][:, c:c + J], EWI[:, e, f * 128:f * 128 + 128],
                                           XG[:, e * J:e * J + J], start=True, stop=True)
                    mm.then_inc(t_ez, 1)

                def expert_out(i):
                    pe.wait_ge(v_h, r * NP + (i + 1))
                    for a in range(2):
                        for f in range(FT):
                            mm = pe.matmul(bank[3 - i // 2][J * a:J * a + J, 128 * (i % 2):128 * (i % 2) + 128],
                                           HE[:, i, a, f, :], EWO[:, 2 * i + a, f, :], start=(f == 0),
                                           stop=(f == FT - 1))
                    if i % 2:
                        mm.then_inc(t_y, 1)

                def turn_gather(t):
                    if t >= 2:
                        pe.wait_ge(a_sm, r * B + (t - 1))
                    elif t == 1:
                        pe.wait_ge(v_w, r * 3 + 2)
                    for p in range(NP):
                        mm = pe.transpose(bank[t % 2][:, 64 * p:64 * p + 64].bitcast(f16),
                                          GM[:, t, 2 * p:2 * p + 2, :].rearrange("p e j -> p (e j)"), identh[:, :])
                    mm.then_inc(t_tr, 1)

                for i in range(NP):
                    expert_in(i)
                    turn_gather(i)
                for i in range(NP):
                    expert_out(i)
                    turn_gather(NP + i)
                for k in range(2):
                    pe.wait_ge(v_y, r * 4 + (2 * k + 2))
                    for t in range(B):
                        if k == 0:
                            pe.wait_ge(a_sm, r * B + (t + 1))
                        for p in range(2 * k, 2 * k + 2):
                            for part in range(3):
                                first = k == 0 and t % 4 == 0 and p == 0 and part == 0
                                mm = pe.matmul(bank[4 + t // 4][:, tok(t % 4)], SM[:, t, p, :], YS[:, part, p, :],
                                               start=first, stop=(p == NP - 1 and part == 2), skip_group_check=True)
                        if k == 1 and t % 4 == 3:
                            mm.then_inc(t_sc, 1)


def kernel(**inputs):
    import numpy as _np
    import concourse.bacc as _bacc
    from concourse import mybir as _mybir
    from concourse.bass_utils import run_bass_kernel_spmd as _run

    def arr(name):
        return _np.asarray(inputs[name])

    cols, width = pack_columns()
    pack = _np.zeros((128, width), _np.float32)

    def put(name, a):
        lo, hi = cols[name]
        pack[:a.shape[0], lo:hi] = a.reshape(a.shape[0], hi - lo)

    p = _np.arange(128)
    put("ident", _np.eye(128, dtype=_np.float32))
    put("before", _np.triu(_np.ones((128, 128), _np.float32), 1))
    slot = _np.where(p < 96, (p % 32) // 8, p % 4)
    put("slot_mask", (slot[:, None] == _np.arange(4)[None, :]).astype(_np.float32))
    put("iota_j", _np.broadcast_to(_np.arange(64, dtype=_np.float32), (128, 64)))
    put("iota_e", _np.broadcast_to(_np.arange(8, dtype=_np.float32), (128, 8)))
    own = _np.zeros((128, 4, 3, 8), _np.float32)
    for pair in range(4):
        own[p, pair, :, 2 * pair + p // 64] = 1.0
    put("own_e", own)

    put("wq", arr("L0_xattn_Wq").T)
    put("wk", arr("L0_xattn_Wk").T)
    spread = (32 * _np.arange(4)[:, None] + _np.arange(96)[None, :] % 32)
    for name, key in (("k3", "k"), ("q3", "q")):
        put("w" + name, arr("L0_xattn_W" + key).T[:, spread.reshape(-1)])
        put("b" + name, arr("L0_xattn_b" + key)[spread].T)
    put("wv", arr("L0_xattn_Wv").T)
    put("wo", arr("L0_xattn_Wo").T)
    put("bq", arr("L0_xattn_bq").reshape(128, 1))
    put("bk", arr("L0_xattn_bk").reshape(128, 1))
    for name, key in (("bv", "L0_xattn_bv"), ("bo", "L0_xattn_bo"), ("gbo", "L0_ffn_gate_bo")):
        put(name, _np.broadcast_to(arr(key), (128, 128)))
    put("gbi", arr("L0_ffn_gate_bi").reshape(4, 128).T)
    put("ebi", arr("L0_ffn_exp_bi").reshape(8, 4, 128).transpose(2, 0, 1))
    put("ebo", _np.repeat(arr("L0_ffn_exp_bo").reshape(4, 2, 128).transpose(1, 0, 2), 64, axis=0))

    c = _np.ascontiguousarray
    arrays = {
        "in_x": c(arr("x").transpose(1, 0, 2)),
        "in_ctxT": c(arr("ctx_1024").reshape(1024, 128).T),
        "in_mask": c(arr("mask_Bx1xSxS2_bk1").reshape(8, 128, 128).transpose(1, 0, 2)),
        "in_pack": pack,
        "in_gwi": c(arr("L0_ffn_gate_wi")),
        "in_gwo": c(arr("L0_ffn_gate_wo").reshape(4, 128, 128).transpose(1, 0, 2)),
        "in_ewi": c(arr("L0_ffn_exp_wi").transpose(1, 0, 2)),
        "in_ewo": c(arr("L0_ffn_exp_wo").reshape(8, 4, 128, 128).transpose(2, 0, 1, 3)),
    }
    nc = _bacc.Bacc("TRN2", target_bir_lowering=False, num_devices=1)
    args = [nc.dram_tensor(n, a.shape, _mybir.dt.from_np(a.dtype), kind="ExternalInput").ap() for n, a in arrays.items()]
    args.append(nc.dram_tensor("out_0", (128, 8, 128), _mybir.dt.float32, kind="ExternalOutput").ap())
    xattn_moe(nc, *args)
    r = _run(nc, [arrays], core_ids=[0])
    return c(r.results[0]["out_0"].transpose(1, 0, 2))
```
